# Optimizing a Trainium2 kernel written in Bass

```python
import numpy as np
import jax
import jax.numpy as jnp

def _softmax(x, axis=-1):
    return jax.nn.softmax(x, axis=axis)

def _gelu(x):
    return jax.nn.gelu(x, approximate=True)

def _silu(x):
    return jax.nn.silu(x)

def _sigmoid(x):
    return jax.nn.sigmoid(x)

def _layernorm(x, axis=-1, eps=1e-05):
    m = jnp.mean(x, axis=axis, keepdims=True)
    v = jnp.var(x, axis=axis, keepdims=True)
    return (x - m) / jnp.sqrt(v + eps)

def _scatter_add(tgt, idx, src, axis=0):
    return tgt.at[idx].add(src)

def _segment_sum(src, seg, n):
    return jax.ops.segment_sum(src, seg, n)
kernel_name = 'mk_adaln_d1_jaxref_r4_f00bca'

def setup_inputs(seed: int=0):
    np.random.seed(seed)
    _w = jnp.asarray

    def _L0_attn_setup():
        import jax, jax.numpy as jnp
        import numpy as np
        EPS = 1e-08

        def _combine(c1, c2):
            a1, b1 = c1
            a2, b2 = c2
            return (a1 * a2, a2 * b1 + b2)
        key = jax.random.key(seed)
        ks = jax.random.split(key, 5)
        B, S, D = (4, 512, 256)
        H = 2 * D
        x = jax.random.normal(ks[0], (B, S, D), dtype=jnp.float32)
        rms_scale = jnp.ones((D,), dtype=jnp.float32)
        split_scale = jax.random.uniform(ks[1], (D,), dtype=jnp.float32)
        W_K = jax.random.normal(ks[2], (D, H), dtype=jnp.float32) * D ** (-0.5)
        W_ugg = jax.random.normal(ks[3], (D, 3 * H), dtype=jnp.float32) * D ** (-0.5)
        W_out = jax.random.normal(ks[4], (H, D), dtype=jnp.float32) * H ** (-0.5)
        return {'x': x, 'rms_scale': rms_scale, 'split_scale': split_scale, 'W_K': W_K, 'W_ugg': W_ugg, 'W_out': W_out}
    _L0_attn_in = _L0_attn_setup()

    def _L0_ffn_setup():
        import jax, jax.numpy as jnp
        import numpy as np
        N_EMBED = 256
        FFN_HIDDEN = 1024
        NUM_EXPERTS = 8
        TOP_K = 2
        key = jax.random.key(seed)
        ks = jax.random.split(key, 8)
        d, f, E = (N_EMBED, FFN_HIDDEN, NUM_EXPERTS)
        s_d = 1.0 / np.sqrt(d)
        s_f = 1.0 / np.sqrt(f)
        return {'x': jax.random.normal(ks[0], (2, 512, d), dtype=jnp.float32), 'Wg': jax.random.uniform(ks[1], (d, E), jnp.float32, -s_d, s_d), 'bg': jax.random.uniform(ks[2], (E,), jnp.float32, -s_d, s_d), 'W1': jax.random.uniform(ks[3], (E, d, f), jnp.float32, -s_d, s_d), 'b1': jax.random.uniform(ks[4], (E, f), jnp.float32, -s_d, s_d), 'W2': jax.random.uniform(ks[5], (E, f, d), jnp.float32, -s_f, s_f), 'b2': jax.random.uniform(ks[6], (E, d), jnp.float32, -s_f, s_f)}
    _L0_ffn_in = _L0_ffn_setup()
    _L0_c = _w((lambda *s: np.random.randn(*s).astype(np.float32) * 0.05)(4, 256))
    _L0_wmod = _w((lambda *s: np.random.randn(*s).astype(np.float32) * 0.05)(256, 6 * 256) * 256 ** (-0.5))
    _d = {'L0_attn_x': _L0_attn_in['x'], 'L0_attn_rms_scale': _L0_attn_in['rms_scale'], 'L0_attn_split_scale': _L0_attn_in['split_scale'], 'L0_attn_W_K': _L0_attn_in['W_K'], 'L0_attn_W_ugg': _L0_attn_in['W_ugg'], 'L0_attn_W_out': _L0_attn_in['W_out'], 'L0_ffn_Wg': _L0_ffn_in['Wg'], 'L0_ffn_bg': _L0_ffn_in['bg'], 'L0_ffn_W1': _L0_ffn_in['W1'], 'L0_ffn_b1': _L0_ffn_in['b1'], 'L0_ffn_W2': _L0_ffn_in['W2'], 'L0_ffn_b2': _L0_ffn_in['b2'], 'L0_c': _L0_c, 'L0_wmod': _L0_wmod}
    _x0 = _d['L0_attn_x']
    _d['L0_attn_x'] = jax.random.normal(jax.random.fold_in(jax.random.key(seed), 1), (4, 1024, 256), dtype=_x0.dtype)
    del _x0
    return _d

def reference(L0_attn_x, L0_attn_rms_scale, L0_attn_split_scale, L0_attn_W_K, L0_attn_W_ugg, L0_attn_W_out, L0_ffn_Wg, L0_ffn_bg, L0_ffn_W1, L0_ffn_b1, L0_ffn_W2, L0_ffn_b2, L0_c, L0_wmod):

    def _L0_attn_ref(x, rms_scale, split_scale, W_K, W_ugg, W_out):
        import jax, jax.numpy as jnp
        import numpy as np
        EPS = 1e-08

        def _combine(c1, c2):
            a1, b1 = c1
            a2, b2 = c2
            return (a1 * a2, a2 * b1 + b2)
        B, S, D = x.shape
        residual = x
        norm = jnp.linalg.norm(x, axis=-1, keepdims=True) * D ** (-0.5)
        xn = rms_scale * x / (norm + EPS) * split_scale
        K = jax.nn.sigmoid(xn @ W_K)
        u, g_in, g_out = jnp.split(xn @ W_ugg, 3, axis=-1)
        u = u * jax.nn.sigmoid(g_in) * (1.0 - K)
        g_out = jax.nn.sigmoid(g_out)
        Kshift = jnp.concatenate([jnp.zeros_like(K[:, :1]), K[:, :-1]], axis=1)
        _, outputs = jax.lax.associative_scan(_combine, (Kshift, u), axis=1)
        y = outputs * g_out @ W_out
        return y + residual

    def _L0_ffn_ref(x, Wg, bg, W1, b1, W2, b2):
        import jax, jax.numpy as jnp
        import numpy as np
        N_EMBED = 256
        FFN_HIDDEN = 1024
        NUM_EXPERTS = 8
        TOP_K = 2
        gate_scores = jax.nn.softmax(x @ Wg + bg, axis=-1)
        topk_scores, topk_idx = jax.lax.top_k(gate_scores, TOP_K)
        topk_scores = topk_scores / (jnp.sum(topk_scores, axis=-1, keepdims=True) + 1e-08)
        onehot = jax.nn.one_hot(topk_idx, NUM_EXPERTS, dtype=x.dtype)
        combine_w = jnp.einsum('bsk,bske->bse', topk_scores, onehot)
        output = jnp.zeros_like(x)
        for e in range(NUM_EXPERTS):
            h = jax.nn.gelu(x @ W1[e] + b1[e])
            y = h @ W2[e] + b2[e]
            output = output + y * combine_w[..., e:e + 1]
        return output
    x = L0_attn_x
    mod = (_silu(L0_c) @ L0_wmod).reshape(L0_c.shape[0], 6, 1, -1)
    sa, ca, ga, sb, cb, gb = (mod[:, 0], mod[:, 1], mod[:, 2], mod[:, 3], mod[:, 4], mod[:, 5])
    ga = (2 * (ga >= 0) - 1) * jnp.maximum(jnp.abs(ga), 0.25)
    gb = (2 * (gb >= 0) - 1) * jnp.maximum(jnp.abs(gb), 0.25)
    h = _layernorm(x, axis=-1) * (1 + ca) + sa
    x = x + ga * _L0_attn_ref(h, L0_attn_rms_scale, L0_attn_split_scale, L0_attn_W_K, L0_attn_W_ugg, L0_attn_W_out)
    h = _layernorm(x, axis=-1) * (1 + cb) + sb
    x = x + gb * _L0_ffn_ref(h, L0_ffn_Wg, L0_ffn_bg, L0_ffn_W1, L0_ffn_b1, L0_ffn_W2, L0_ffn_b2)
    return x

_drawn_inputs = setup_inputs


def setup_inputs(seed=0):
    import zlib

    import numpy as np

    out = dict(_drawn_inputs(seed))
    spreads = {'L0_attn_rms_scale': (1.0, 0.6)}
    factors = {'L0_attn_split_scale': 4.433,
     'L0_attn_W_K': 8.0,
     'L0_ffn_bg': 8.0,
     'L0_ffn_b1': 25.42,
     'L0_ffn_b2': 8.0}
    for name, (base, spread) in spreads.items():
        noise = np.random.default_rng([zlib.crc32(name.encode()), seed]).standard_normal(out[name].shape)
        drawn = base * np.exp(spread * noise) if base else spread * noise
        out[name] = jnp.asarray(drawn.astype(out[name].dtype))
    for name, factor in factors.items():
        out[name] = (out[name] * factor).astype(out[name].dtype)
    return out
```

```python
from contextlib import ExitStack

import concourse.bass as bass
from concourse import mybir

F32 = mybir.dt.float32
F32R = mybir.dt.float32r
I32 = mybir.dt.int32
ALU = mybir.AluOpType
ACT = mybir.ActivationFunctionType
AX = mybir.AxisListType.X

D = 256
H = 512
E = 8
FF = 1024
NF = FF // 128
T = 512
NG = 8
NB = 4
TOK = NG * T
CAP = TOK
MAGIC = 0x5F3759DF


def build(nc, x, rms, split, W_K, W_ugg, W_out, Wg, bg, W1, b1, W2, b2, c, wmod, out):
    x_rows = x.rearrange("b s d -> (b s) d")
    out_rows = out.rearrange("b s d -> (b s) d")
    Xd = nc.dram_tensor("disp_x", (E * CAP, D), F32, kind="Internal").ap()
    Yd = nc.dram_tensor("disp_y", (2 * TOK + T, D), F32, kind="Internal").ap()
    x2d = nc.dram_tensor("x2_rows", (TOK, D), F32, kind="Internal").ap()
    modd = nc.dram_tensor("mod_rows", (NB, 6 * D), F32, kind="Internal").ap()

    def rows(t, g):
        return t[g * T:(g + 1) * T, :].rearrange("(j p) d -> p j d", p=128)

    with ExitStack() as ctx:
        def sem(name):
            return ctx.enter_context(nc.semaphore(name))

        def sb(stack, name, shape, dt=F32):
            return stack.enter_context(nc.sbuf_tensor(name, shape, dt))

        h2all = sb(ctx, "h2all", [128, 4 * NG, D])
        wraw = sb(ctx, "wraw", [128, 4096])
        mb = sb(ctx, "mb", [128, 2, 6 * D])
        x2b = sb(ctx, "x2b", [128, 2, 4, D])
        ident = sb(ctx, "ident", [128, 128])
        upper = sb(ctx, "upper", [128, 128])
        ones = sb(ctx, "ones", [128, 128])
        zcol = sb(ctx, "zcol", [128, 1])
        vrow = sb(ctx, "vrow", [76, 128])
        vT = sb(ctx, "vT", [128, 76])
        sv = sb(ctx, "sv", [128, 2])
        sgc = sb(ctx, "sgc", [128, 8])
        scT = sb(ctx, "scT", [128, 2, NB])
        wg = sb(ctx, "wg", [128, 2, E])
        bgb = sb(ctx, "bgb", [128, E])
        ioi = sb(ctx, "ioi", [128, 160], I32)
        iof = sb(ctx, "iof", [128, 160])
        bst = sb(ctx, "bst", [128, 4, 6])
        mv = sb(ctx, "mv", [128, 4, 2])
        nt = sb(ctx, "nt", [128, 6, 4])
        rsn = sb(ctx, "rsn", [128, 2, 2, 4])
        ss = sb(ctx, "ss", [128, 2, 4])
        rin = sb(ctx, "rin", [128, 2, 4])
        rsn2 = sb(ctx, "rsn2", [128, 2, 2, 4])
        Lall = sb(ctx, "Lall", [128, 4 * NG, E])
        mx1 = sb(ctx, "mx1", [128, 4 * NG])
        mx2 = sb(ctx, "mx2", [128, 4 * NG])
        rt = sb(ctx, "rt", [128, 4, 4, E])
        rmin = sb(ctx, "rmin", [128, 4])
        sel = sb(ctx, "sel", [128, 2, 4 * NG, E])
        selb = sb(ctx, "selb", [128, 4, E])
        csum = sb(ctx, "csum", [128, E])
        posf = sb(ctx, "posf", [128, 2, 4])
        pos = sb(ctx, "pos", [128, 2, 4 * NG], I32)
        posy = sb(ctx, "posy", [128, 2, 4 * NG], I32)
        yoff = sb(ctx, "yoff", [128, 3, E])
        yoint = sb(ctx, "yoint", [128, E], I32)
        nf = sb(ctx, "nf", [128, E])
        ncmp = sb(ctx, "ncmp", [128, E, 7])
        kf = sb(ctx, "kf", [128, E])
        kint = sb(ctx, "kint", [128, E], I32)
        nmint = sb(ctx, "nmint", [128, E], I32)
        cw = sb(ctx, "cw", [128, 4, 4 * NG])

        tp = [ctx.enter_context(nc.psum_tensor(f"tp{i}", [128, 512], F32)) for i in range(2)]
        mm = [ctx.enter_context(nc.psum_tensor(f"mm{i}", [128, 512], F32)) for i in range(4)]
        yb = [ctx.enter_context(nc.psum_tensor(f"yb{i}", [128, 512], F32)) for i in range(2)]

        with ExitStack() as p1:
            WH = sb(p1, "WH", [128, 2, 2048], F32R)
            WL = sb(p1, "WL", [128, 2, 2048], F32R)
            WOH = sb(p1, "WOH", [128, 4, D], F32R)
            WOL = sb(p1, "WOL", [128, 4, D], F32R)
            xb = sb(p1, "xb", [128, 2, 4, D])
            hb = sb(p1, "hb", [128, 3, 4, D])
            zb = sb(p1, "zb", [128, 4, D])
            xnb = sb(p1, "xnb", [128, 4, D])
            xh = sb(p1, "xh", [128, 2, 2, T], F32R)
            xl = sb(p1, "xl", [128, 2, 2, T], F32R)
            kb = sb(p1, "kb", [128, 4, T + 1])
            sgi = sb(p1, "sgi", [128, 2, T])
            sgo = sb(p1, "sgo", [128, 2, T])
            ub = sb(p1, "ub", [128, 2, T])
            wb = sb(p1, "wb", [128, T])
            ob = sb(p1, "ob", [128, 2, T])
            cy = sb(p1, "cy", [128, 4])
            og = sb(p1, "og", [128, 2, T])
            oh = sb(p1, "oh", [128, 3, T], F32R)
            ol = sb(p1, "ol", [128, 3, T], F32R)
            h2T = sb(p1, "h2T", [128, 2, T])
        with ExitStack() as p2:
            SH = [None, None]
            SL = [None, None]
            for i in range(2):
                SH[i] = sb(p2, f"SH{i}", [128, 4096], F32R)
                SL[i] = sb(p2, f"SL{i}", [128, 4096], F32R)
            xin = sb(p2, "xin", [128, 4, D])
            fh = sb(p2, "fh", [128, 2, T], F32R)
            fl = sb(p2, "fl", [128, 2, T], F32R)
            h32 = sb(p2, "h32", [128, 2, T])
            hh = sb(p2, "hh", [128, NF, T], F32R)
            hl = sb(p2, "hl", [128, NF, T], F32R)
            ysb = sb(p2, "ysb", [128, 4, D])
            b1T = sb(p2, "b1T", [128, E * NF])
            b2b = sb(p2, "b2b", [128, E, D])
        with ExitStack() as p3:
            ga_ = sb(p3, "gat_a", [128, 2, 4, D])
            gb_ = sb(p3, "gat_b", [128, 2, 4, D])
            x2r = sb(p3, "x2r", [128, 2, 4, D])
            gbb = sb(p3, "gbb", [128, NB, D])
            ores = sb(p3, "ores", [128, 2, 4, D])

        exd = mb[:, 0, 0:4 * NG * E].rearrange("p (t e) -> p t e", e=E)
        exd2 = mb[:, 1, 0:4 * NG]
        x2f = x2b[:, :, :, :].rearrange("p a j d -> p (a j d)")
        modr = x2f[0:NB, 0:6 * D]
        mtmp = x2f[0:NB, 6 * D:8 * D].rearrange("p (a d) -> p a d", a=2)
        wmod_sb = h2all[:, 0:12, :].rearrange("p a d -> p (a d)").rearrange("p (c n) -> p c n", c=2)
        wo_raw = h2all[:, 12:16, :]
        zfill = h2all[:, 28:32, :]
        wat = wraw[:, :].rearrange("p (c n) -> p c n", c=2)
        em8 = iof[:, 0:32].rearrange("p (j e) -> p j e", j=4)
        ebase = iof[:, 32:64].rearrange("p (j e) -> p j e", j=4)
        thr = iof[:, 64:120].rearrange("p (e m) -> p e m", e=E)

        names = ("xa", "xb_", "wa", "wo", "wmod", "vec", "gat", "b2", "cst", "iota", "vT", "vTc", "sgc", "scT", "sv",
                 "mod", "modr", "modw", "mb0", "mb1", "zs", "zf", "wh", "wl", "woh", "wol", "b1T",
                 "s1", "z", "h", "sq", "r", "xn", "xt", "xh", "xl", "bas", "mm", "sg", "k", "so", "u", "w", "sc",
                 "og", "oh", "ol", "cy", "y", "t1", "x2", "x2w0", "x2w1", "s2", "z2", "h2", "ht", "he", "lg", "m",
                 "rk", "pos", "scat", "nc", "kr", "ch", "ach", "pch", "e1", "e2", "cw", "raw", "sph", "spl",
                 "xin", "tp2", "fh", "fl", "l1", "g", "hlo", "l2", "yev", "yst", "yf", "fin",
                 "ga0", "ga1", "gs", "xr0", "xr1", "gbb", "ft", "fo", "ou0", "ou1")
        S = {n: sem("s_" + n) for n in names}

        def w(eng, name, n):
            if n > 0:
                eng.wait_ge(S[name], n)

        def bc(ap, j):
            return ap.unsqueeze(1).to_broadcast([128, j, ap.shape[-1]])

        steps = []

        def step(engine):
            def add(fn):
                steps.append((engine, fn))
                return fn
            return add

        count = {"ch": 0, "ach": 0, "pch": 0}

        def link(eng, ins, name="ch"):
            count[name] += 1
            ins.then_inc(S[name], 1)
            eng.wait_ge(S[name], count[name])

        def mod(b, n):
            return mb[:, b % 2, n * D:(n + 1) * D]

        def rsqrt(v, y, a):
            def run(e):
                link(e, e.tensor_scalar(a.bitcast(I32), v.bitcast(I32), 1, None, ALU.logical_shift_right))
                link(e, e.tensor_scalar(y.bitcast(I32), a.bitcast(I32), -1, MAGIC, ALU.mult, ALU.add))
                for _ in range(3):
                    link(e, e.tensor_tensor(a, y, y, ALU.mult))
                    link(e, e.scalar_tensor_tensor(a, a, -0.5, v, ALU.mult, ALU.mult))
                    link(e, e.scalar_tensor_tensor(y, a, 1.5, y, ALU.add, ALU.mult))
            return run

        def setup():
            @step("sp")
            def _(e):
                for t, (src, n) in enumerate(((b1.rearrange("e (f p) -> (e f) p", p=128), 64),
                                              (rms.rearrange("(c p) -> c p", p=128), 2),
                                              (split.rearrange("(c p) -> c p", p=128), 2),
                                              (c.rearrange("b (c p) -> (b c) p", p=128), 8))):
                    r0 = (0, 64, 66, 68)[t]
                    e.dma_start(vrow[r0:r0 + n, :], src).then_inc(S["vec"], 16)
                e.dma_start(wmod_sb, wmod.rearrange("(c p) n -> p c n", p=128)).then_inc(S["wmod"], 16)
                e.dma_start(xb[:, 0, :, :], rows(x_rows, 0)).then_inc(S["xa"], 16)
                e.dma_start(wat[:, :, 0:H], W_K.rearrange("(c p) n -> p c n", p=128)).then_inc(S["wa"], 16)
                e.dma_start(wat[:, :, H:4 * H], W_ugg.rearrange("(c p) n -> p c n", p=128)).then_inc(S["wa"], 16)
                e.dma_start(wo_raw, W_out.rearrange("(c p) n -> p c n", p=128)).then_inc(S["wo"], 16)
                e.dma_start(wg[:, :, :], Wg.rearrange("(c p) n -> p c n", p=128)).then_inc(S["gat"], 16)
                e.dma_start(bgb[:, :], bg.partition_broadcast(128)).then_inc(S["gat"], 16)
                e.dma_start(xb[:, 1, :, :], rows(x_rows, 1)).then_inc(S["xb_"], 16)
                w(e, "modr", 1)
                e.dma_start(modd, modr).then_inc(S["modw"], 16)
                w(e, "modw", 16)
                for b in range(2):
                    e.dma_start(mb[:, b, :], modd[b, :].partition_broadcast(128)).then_inc(S[f"mb{b}"], 16)
                w(e, "zs", 1)
                for n in range(E):
                    e.dma_start(Xd[n * CAP:n * CAP + T, :].rearrange("(j p) d -> p j d", p=128), zfill)\
                        .then_inc(S["zf"], 16)
                e.dma_start(Yd[2 * TOK:2 * TOK + T, :].rearrange("(j p) d -> p j d", p=128), zfill)\
                    .then_inc(S["zf"], 16)
                w(e, "wl", 2)
                load_expert(e, 0)

            @step("pool")
            def _(e):
                e.memset(ident[:, :], 0.0).then_inc(S["cst"], 1)
                e.memset(upper[:, :], 1.0).then_inc(S["cst"], 1)
                e.memset(ones[:, :], 1.0).then_inc(S["cst"], 1)
                e.memset(zcol[:, :], 0.0).then_inc(S["cst"], 1)
                e.wait_ge(S["cst"], 4)
                e.affine_select(out=ident[:, :], in_=ident[:, :], compare_op=ALU.not_equal, fill=1.0, base=0,
                                pattern=[[-1, 128]], channel_multiplier=1).then_inc(S["cst"], 1)
                e.affine_select(out=upper[:, :], in_=upper[:, :], compare_op=ALU.is_gt, fill=0.0, base=0,
                                pattern=[[1, 128]], channel_multiplier=-1).then_inc(S["cst"], 1)
                e.memset(csum[:, :], 0.0).then_inc(S["cst"], 1)
                e.memset(zfill, 0.0).then_inc(S["zs"], 1)
                e.iota(ioi[:, 0:32].rearrange("p (j e) -> p j e", j=4), [[0, 4], [1, E]], base=-8,
                       channel_multiplier=0).then_inc(S["iota"], 1)
                e.iota(ioi[:, 32:64].rearrange("p (j e) -> p j e", j=4), [[0, 4], [CAP, E]], base=0,
                       channel_multiplier=0).then_inc(S["iota"], 1)
                e.iota(ioi[:, 64:120].rearrange("p (e m) -> p e m", e=E), [[0, E], [T, 7]], base=T,
                       channel_multiplier=0).then_inc(S["iota"], 1)

            @step("pe")
            def _(e):
                w(e, "cst", 6)
                w(e, "vec", 64)
                e.transpose(tp[0][:, 0:76], vrow[:, :], ident[0:76, 0:76]).then_inc(S["vT"], 1)
                w(e, "scT", 1)
                w(e, "wmod", 16)
                for n in range(3):
                    for k in range(2):
                        i = e.matmul(mm[n][0:NB, :], scT[:, k, :], wmod_sb[:, k, n * 512:(n + 1) * 512],
                                     start=(k == 0), stop=(k == 1))
                    i.then_inc(S["mod"], 1)

            @step("act")
            def _(e):
                w(e, "vTc", 1)
                e.activation(sgc[:, :], vT[:, 68:76], ACT.Sigmoid).then_inc(S["sgc"], 1)

            @step("dve")
            def _(e):
                w(e, "vT", 1)
                e.tensor_copy(vT[:, :], tp[0][:, 0:76]).then_inc(S["vTc"], 1)
                w(e, "vTc", 1)
                e.tensor_tensor(sv[:, :], vT[:, 64:66], vT[:, 66:68], ALU.mult).then_inc(S["sv"], 1)
                w(e, "sgc", 1)
                e.tensor_tensor(scT[:, :, :].rearrange("p c b -> p b c"),
                                vT[:, 68:76].rearrange("p (b c) -> p b c", b=NB),
                                sgc[:, :].rearrange("p (b c) -> p b c", b=NB), ALU.mult).then_inc(S["scT"], 1)
                w(e, "iota", 3)
                link(e, e.tensor_copy(iof[:, 0:120], ioi[:, 0:120]))

            @step("act")
            def _(e):
                w(e, "wa", 32)
                w(e, "sv", 1)
                for k in range(2):
                    e.activation(WH[:, k, :], wat[:, k, :], ACT.Copy, scale=sv[:, k:k + 1]).then_inc(S["wh"], 1)
                w(e, "wo", 16)
                e.activation(WOH[:, :, :], wo_raw, ACT.Copy).then_inc(S["woh"], 1)

            @step("dve")
            def _(e):
                w(e, "mod", 3)
                link(e, e.tensor_copy(modr[:, 0:D], mm[0][0:NB, 0:D]))
                link(e, e.tensor_scalar(modr[:, D:2 * D], mm[0][0:NB, D:2 * D], 1.0, None, ALU.add))
                link(e, e.tensor_copy(modr[:, 3 * D:4 * D], mm[1][0:NB, D:2 * D]))
                link(e, e.tensor_scalar(modr[:, 4 * D:5 * D], mm[2][0:NB, 0:D], 1.0, None, ALU.add))
                for src, n in ((mm[1][0:NB, 0:D], 2), (mm[2][0:NB, D:2 * D], 5)):
                    link(e, e.tensor_copy(mtmp[:, 0, :], src))
                    link(e, e.scalar_tensor_tensor(mtmp[:, 1, :], mtmp[:, 0, :], -1.0, mtmp[:, 0, :],
                                                   ALU.mult, ALU.max))
                    link(e, e.tensor_scalar(mtmp[:, 1, :], mtmp[:, 1, :], 0.25, None, ALU.max))
                    link(e, e.tensor_scalar(mtmp[:, 0, :], mtmp[:, 0, :], 0.0, 2.0, ALU.is_ge, ALU.mult))
                    i = e.scalar_tensor_tensor(modr[:, n * D:(n + 1) * D], mtmp[:, 0, :], -1.0, mtmp[:, 1, :],
                                               ALU.add, ALU.mult)
                    if n == 2:
                        link(e, i)
                    else:
                        i.then_inc(S["modr"], 1)
                for k in range(2):
                    w(e, "wh", k + 1)
                    e.scalar_tensor_tensor(WL[:, k, :], wat[:, k, :], sv[:, k:k + 1], WH[:, k, :].bitcast(F32),
                                           ALU.mult, ALU.subtract).then_inc(S["wl"], 1)
                w(e, "woh", 1)
                e.tensor_tensor(WOL[:, :, :], wo_raw, WOH[:, :, :].bitcast(F32), ALU.subtract).then_inc(S["wol"], 1)

        def load_expert(e, n):
            e.dma_start(wraw[:, 0:2048].rearrange("p (c n) -> p c n", c=2),
                        W1[n].rearrange("(c p) n -> p c n", p=128)).then_inc(S["raw"], 16)
            e.dma_start(wraw[:, 2048:4096].rearrange("p (c n) -> p c n", c=NF),
                        W2[n].rearrange("(c p) n -> p c n", p=128)).then_inc(S["raw"], 16)

        def ln1(g):
            b = g // 2

            @step("dve")
            def _(e):
                w(e, ("xa", "xb_")[g % 2], 16 * (g // 2 + 1))
                for j in range(4):
                    i = e.bn_stats(bst[:, j, :], xb[:, g % 2, j, :])
                link(e, i)
                for j in range(4):
                    i = e.bn_aggr(mv[:, j, :], bst[:, j, :])
                link(e, i)
                link(e, e.tensor_scalar(nt[:, 0, :], mv[:, :, 1], 1e-5, None, ALU.add))
                w(e, "z", g - 1)
                rsqrt(nt[:, 0, :], rsn[:, g % 2, 0, :], nt[:, 1, :])(e)
                e.scalar_tensor_tensor(rsn[:, g % 2, 1, :], mv[:, :, 0], -1.0, rsn[:, g % 2, 0, :],
                                       ALU.mult, ALU.mult).then_inc(S["s1"], 1)
                w(e, "s1", g + 1)

            @step("act")
            def _(e):
                w(e, "s1", g + 1)
                w(e, "h", g)
                for j in range(4):
                    i = e.activation(zb[:, j, :], xb[:, g % 2, j, :], ACT.Identity,
                                     scale=rsn[:, g % 2, 0, j:j + 1], bias=rsn[:, g % 2, 1, j:j + 1])
                i.then_inc(S["z"], 1)

            @step("pool")
            def _(e):
                w(e, f"mb{b % 2}", 16 * (b // 2 + 1))
                w(e, "z", g + 1)
                w(e, "x2", g - 2)
                link(e, e.tensor_tensor(hb[:, g % 3, :, :], zb[:, :, :], bc(mod(b, 1), 4), ALU.mult), "pch")
                e.tensor_tensor(hb[:, g % 3, :, :], hb[:, g % 3, :, :], bc(mod(b, 0), 4), ALU.add)\
                    .then_inc(S["h"], 1)

            @step("act")
            def _(e):
                w(e, "h", g + 1)
                w(e, "xt", 2 * g)
                w(e, "r", g - 1)
                for j in range(4):
                    i = e.activation(xnb[:, j, :], hb[:, g % 3, j, :], ACT.Square,
                                     accum_out=ss[:, g % 2, j:j + 1])
                i.then_inc(S["sq"], 1)

            @step("dve")
            def _(e):
                w(e, "sq", g + 1)
                link(e, e.tensor_scalar(nt[:, 2, :], ss[:, g % 2, :], 1.0 / D, 1e-34, ALU.mult, ALU.max))
                rsqrt(nt[:, 2, :], nt[:, 3, :], nt[:, 4, :])(e)
                link(e, e.tensor_tensor(nt[:, 5, :], nt[:, 2, :], nt[:, 3, :], ALU.mult))
                link(e, e.tensor_scalar(nt[:, 5, :], nt[:, 5, :], 1e-8, None, ALU.add))
                w(e, "xn", g - 1)
                e.reciprocal(rin[:, g % 2, :], nt[:, 5, :]).then_inc(S["r"], 1)
                w(e, "r", g + 1)

            @step("act")
            def _(e):
                w(e, "r", g + 1)
                for j in range(4):
                    i = e.activation(xnb[:, j, :], hb[:, g % 3, j, :], ACT.Copy, scale=rin[:, g % 2, j:j + 1])
                i.then_inc(S["xn"], 1)

            @step("pool")
            def _(e):
                w(e, "xn", g + 1)
                link(e, e.tensor_tensor(hb[:, g % 3, :, :], hb[:, g % 3, :, :], bc(mod(b, 2), 4), ALU.mult), "pch")
                e.tensor_tensor(hb[:, g % 3, :, :], hb[:, g % 3, :, :], xb[:, g % 2, :, :], ALU.add)\
                    .then_inc(S["bas"], 1)

            @step("sp")
            def _(e):
                if g + 2 < NG:
                    w(e, "bas", g + 1)
                    e.dma_start(xb[:, g % 2, :, :], rows(x_rows, g + 2)).then_inc(S[("xa", "xb_")[g % 2]], 16)

        def xt(g):
            @step("pe")
            def _(e):
                w(e, "xn", g + 1)
                if g >= 3:
                    w(e, "pos", g - 2)
                if g == 0:
                    w(e, "vTc", 1)
                w(e, "xl", 2 * g)
                w(e, "he", 2 * (g - 2))
                for k in range(2):
                    for j in range(4):
                        i = e.transpose(tp[k][:, j * 128:(j + 1) * 128], xnb[:, j, k * 128:(k + 1) * 128],
                                        ident[:, :])
                    i.then_inc(S["xt"], 1)

            @step("act")
            def _(e):
                for k in range(2):
                    w(e, "xt", 2 * g + k + 1)
                    if g >= 2:
                        w(e, "mm", 16 * (g - 1))
                    e.activation(xh[:, g % 2, k, :], tp[k][:, :], ACT.Copy).then_inc(S["xh"], 1)

            @step("dve")
            def _(e):
                for k in range(2):
                    w(e, "xh", 2 * g + k + 1)
                    e.tensor_tensor(xl[:, g % 2, k, :], tp[k][:, :], xh[:, g % 2, k, :].bitcast(F32), ALU.subtract)\
                        .then_inc(S["xl"], 1)

        KINDS = (("sg", 2), ("u", 1), ("k", 0), ("so", 3))

        def main(g, hc):
            n = 4 * g + hc

            @step("pe")
            def _(e):
                w(e, "xl", 2 * g + 2)
                w(e, "wl", 2)
                if n == 0:
                    w(e, "modr", 1)
                for q, (ev, kind) in enumerate(KINDS):
                    w(e, ev, n)
                    c0 = kind * H + hc * 128
                    i = None
                    for k in range(2):
                        for t, (a, b) in enumerate(((WH, xh), (WH, xl), (WL, xh))):
                            i = e.matmul(mm[q][:, :], a[:, k, c0:c0 + 128], b[:, g % 2, k, :],
                                         start=(k == 0 and t == 0), stop=(k == 1 and t == 2))
                    i.then_inc(S["mm"], 1)

            @step("act")
            def _(e):
                w(e, "mm", 4 * n + 1)
                w(e, "u", n - 1)
                e.activation(sgi[:, n % 2, :], mm[0][:, :], ACT.Sigmoid).then_inc(S["sg"], 1)
                w(e, "sc", n - 3)
                w(e, "k", n - 3)
                link(e, e.activation(kb[:, hc, 0:1], kb[:, hc, T:T + 1] if g % 2 else zcol[:, :], ACT.Copy), "ach")
                w(e, "mm", 4 * n + 3)
                e.activation(kb[:, hc, 1:T + 1], mm[2][:, :], ACT.Sigmoid).then_inc(S["k"], 1)
                w(e, "mm", 4 * n + 4)
                w(e, "og", n - 1)
                e.activation(sgo[:, n % 2, :], mm[3][:, :], ACT.Sigmoid).then_inc(S["so"], 1)

            @step("dve")
            def _(e):
                w(e, "mm", 4 * n + 2)
                w(e, "sg", n + 1)
                e.tensor_tensor(ub[:, n % 2, :], mm[1][:, :], sgi[:, n % 2, :], ALU.mult).then_inc(S["u"], 1)
                w(e, "k", n + 1)
                w(e, "u", n + 1)
                e.scalar_tensor_tensor(wb[:, :], kb[:, hc, 1:T + 1], 1.0, ub[:, n % 2, :], ALU.subtract, ALU.mult)\
                    .then_inc(S["w"], 1)
                w(e, "w", n + 1)
                w(e, "og", n - 1)
                e.tensor_tensor_scan(ob[:, n % 2, :], kb[:, hc, 0:T], wb[:, :],
                                     cy[:, hc:hc + 1] if g % 2 else 0.0, ALU.mult, ALU.add).then_inc(S["sc"], 1)
                w(e, "sc", n + 1)
                if g % 2 == 0:
                    link(e, e.tensor_copy(cy[:, hc:hc + 1], ob[:, n % 2, T - 1:T]))

            @step("pool")
            def _(e):
                w(e, "sc", n + 1)
                w(e, "so", n + 1)
                w(e, "ol", n - 1)
                e.tensor_tensor(og[:, n % 2, :], ob[:, n % 2, :], sgo[:, n % 2, :], ALU.mult).then_inc(S["og"], 1)

        def split_o(g, hc):
            n = 4 * g + hc

            @step("act")
            def _(e):
                w(e, "og", n + 1)
                w(e, "y", n - 2)
                e.activation(oh[:, n % 3, :], og[:, n % 2, :], ACT.Copy).then_inc(S["oh"], 1)

            @step("pool")
            def _(e):
                w(e, "oh", n + 1)
                e.tensor_tensor(ol[:, n % 3, :], og[:, n % 2, :], oh[:, n % 3, :].bitcast(F32), ALU.subtract)\
                    .then_inc(S["ol"], 1)

        def project(g, hc):
            n = 4 * g + hc

            @step("pe")
            def _(e):
                w(e, "ol", n + 1)
                w(e, "wol", 1)
                if hc == 0:
                    w(e, "t1", g)
                for j in range(4):
                    o = yb[j // 2][:, (j % 2) * D:(j % 2 + 1) * D]
                    for t, (a, b) in enumerate(((oh, WOH), (oh, WOL), (ol, WOH))):
                        i = e.matmul(o, a[:, n % 3, j * 128:(j + 1) * 128], b[:, hc, :],
                                     start=(hc == 0 and j % 2 == 0 and t == 0), stop=(hc == 3 and t == 2),
                                     skip_group_check=True)
                i.then_inc(S["y"], 1)

        def post(g):
            b = g // 2

            @step("dve")
            def _(e):
                w(e, "y", 4 * g + 4)
                w(e, "modw", 16)
                w(e, f"x2w{g % 2}", 16 * (g // 2))
                w(e, "z2", g - 1)
                for q in range(2):
                    i = e.tensor_tensor(x2b[:, g % 2, 2 * q:2 * q + 2, :],
                                        yb[q][:, :].rearrange("p (j d) -> p j d", j=2), bc(mod(b, 2), 2), ALU.mult)
                i.then_inc(S["t1"], 1)

            @step("pool")
            def _(e):
                w(e, "t1", g + 1)
                w(e, "bas", g + 1)
                e.tensor_tensor(x2b[:, g % 2, :, :], hb[:, g % 3, :, :], x2b[:, g % 2, :, :], ALU.subtract)\
                    .then_inc(S["x2"], 1)

            @step("sp")
            def _(e):
                w(e, "x2", g + 1)
                e.dma_start(rows(x2d, g), x2b[:, g % 2, :, :]).then_inc(S[f"x2w{g % 2}"], 16)

        def ln2(g):
            b = g // 2

            @step("dve")
            def _(e):
                w(e, "x2", g + 1)
                for j in range(4):
                    i = e.bn_stats(bst[:, j, :], x2b[:, g % 2, j, :])
                link(e, i)
                for j in range(4):
                    i = e.bn_aggr(mv[:, j, :], bst[:, j, :])
                link(e, i)
                link(e, e.tensor_scalar(nt[:, 0, :], mv[:, :, 1], 1e-5, None, ALU.add))
                w(e, "z2", g - 1)
                rsqrt(nt[:, 0, :], rsn2[:, g % 2, 0, :], nt[:, 1, :])(e)
                e.scalar_tensor_tensor(rsn2[:, g % 2, 1, :], mv[:, :, 0], -1.0, rsn2[:, g % 2, 0, :],
                                       ALU.mult, ALU.mult).then_inc(S["s2"], 1)
                w(e, "s2", g + 1)

            @step("act")
            def _(e):
                w(e, "s2", g + 1)
                w(e, "wol", 1)
                w(e, "zf", 16 * (E + 1))
                for j in range(4):
                    i = e.activation(h2all[:, 4 * g + j, :], x2b[:, g % 2, j, :], ACT.Identity,
                                     scale=rsn2[:, g % 2, 0, j:j + 1], bias=rsn2[:, g % 2, 1, j:j + 1])
                i.then_inc(S["z2"], 1)

            @step("pool")
            def _(e):
                w(e, "z2", g + 1)
                hv = h2all[:, 4 * g:4 * g + 4, :]
                link(e, e.tensor_tensor(hv, hv, bc(mod(b, 4), 4), ALU.mult), "pch")
                e.tensor_tensor(hv, hv, bc(mod(b, 3), 4), ALU.add).then_inc(S["h2"], 1)

            @step("sp")
            def _(e):
                if g % 2 and b + 2 < NB:
                    w(e, "h2", g + 1)
                    e.dma_start(mb[:, b % 2, :], modd[b + 2, :].partition_broadcast(128))\
                        .then_inc(S[f"mb{b % 2}"], 16)

        def turn_h(g):
            @step("pe")
            def _(e):
                w(e, "h2", g + 1)
                w(e, "xl", 2 * min(g + 3, NG))
                w(e, "pos", g)
                for k in range(2):
                    for j in range(4):
                        i = e.transpose(tp[k][:, j * 128:(j + 1) * 128],
                                        h2all[:, 4 * g + j, k * 128:(k + 1) * 128], ident[:, :])
                    i.then_inc(S["ht"], 1)

            @step("act")
            def _(e):
                w(e, "lg", g)
                for k in range(2):
                    w(e, "ht", 2 * g + k + 1)
                    e.activation(h2T[:, k, :], tp[k][:, :], ACT.Copy).then_inc(S["he"], 1)

        def logits(g):
            @step("pe")
            def _(e):
                w(e, "he", 2 * g + 2)
                w(e, "gat", 32)
                for j in range(4):
                    for k in range(2):
                        i = e.matmul(tp[0][:, j * E:(j + 1) * E], h2T[:, k, j * 128:(j + 1) * 128], wg[:, k, :],
                                     start=(k == 0), stop=(k == 1))
                i.then_inc(S["lg"], 1)

            @step("dve")
            def _(e):
                w(e, "lg", g + 1)
                Lg = Lall[:, 4 * g:4 * g + 4, :]
                m1 = mx1[:, 4 * g:4 * g + 4]
                m2 = mx2[:, 4 * g:4 * g + 4]
                sel1, sel2 = (sel[:, q, 4 * g:4 * g + 4, :] for q in range(2))

                def wide(v):
                    return v.unsqueeze(2).to_broadcast([128, 4, E])

                def first(src, mx, to):
                    link(e, e.tensor_tensor(rt[:, 0, :, :], src, wide(mx), ALU.is_equal))
                    link(e, e.tensor_tensor(rt[:, 0, :, :], rt[:, 0, :, :], em8, ALU.mult))
                    link(e, e.tensor_reduce(rmin[:, :], rt[:, 0, :, :], AX, ALU.min))
                    link(e, e.tensor_tensor(to, em8, wide(rmin[:, :]), ALU.is_equal))

                link(e, e.tensor_tensor(Lg, tp[0][:, 0:4 * E].rearrange("p (j e) -> p j e", j=4), bc(bgb[:, :], 4),
                                        ALU.add))
                link(e, e.tensor_reduce(m1, Lg, AX, ALU.max))
                first(Lg, m1, sel1)
                link(e, e.scalar_tensor_tensor(rt[:, 1, :, :], sel1, -3e38, Lg, ALU.mult, ALU.add))
                link(e, e.tensor_reduce(m2, rt[:, 1, :, :], AX, ALU.max))
                first(rt[:, 1, :, :], m2, sel2)
                e.tensor_tensor(selb[:, :, :], sel1, sel2, ALU.add).then_inc(S["m"], 1)
                w(e, "m", g + 1)

        def rank(g):
            @step("pe")
            def _(e):
                w(e, "m", g + 1)
                w(e, "cst", 7)
                flat = selb[:, :, :].rearrange("p j e -> p (j e)")
                o = tp[0]
                e.matmul(o[:, 128:160], upper[:, :], flat, start=True, stop=False, skip_group_check=True)
                for q in range(1, 4):
                    e.matmul(o[:, 128 + E * q:160], ones[:, :], flat[:, 0:E * (4 - q)], start=False, stop=False,
                             skip_group_check=True)
                e.matmul(o[:, 128:160], ones[:, :], bc(csum[:, :], 4), start=False, stop=True,
                         skip_group_check=True).then_inc(S["rk"], 1)

            @step("dve")
            def _(e):
                w(e, "rk", g + 1)
                sel1, sel2 = (sel[:, q, 4 * g:4 * g + 4, :] for q in range(2))
                link(e, e.tensor_tensor(rt[:, 2, :, :], tp[0][:, 128:160].rearrange("p (j e) -> p j e", j=4), ebase,
                                        ALU.add))
                link(e, e.tensor_tensor(rt[:, 3, :, :], rt[:, 2, :, :], sel1, ALU.mult))
                link(e, e.tensor_reduce(posf[:, 0, :], rt[:, 3, :, :], AX, ALU.add))
                link(e, e.tensor_tensor(rt[:, 3, :, :], rt[:, 2, :, :], sel2, ALU.mult))
                link(e, e.tensor_reduce(posf[:, 1, :], rt[:, 3, :, :], AX, ALU.add))
                e.tensor_copy(pos[:, :, 4 * g:4 * g + 4], posf[:, :, :]).then_inc(S["pos"], 1)
                link(e, e.tensor_reduce(kf[:, :], selb[:, :, :].rearrange("p j e -> p e j"), AX, ALU.add))
                link(e, e.tensor_tensor(csum[:, :], csum[:, :], kf[:, :], ALU.add))

        def scatter(g):
            @step("pool")
            def _(e):
                w(e, "pos", g + 1)
                w(e, "zf", 16 * (E + 1))
                for j in range(4 * g, 4 * g + 4):
                    for p in (pos[:, 0, :], pos[:, 1, :]):
                        e.indirect_dma_start(out=Xd, out_offset=bass.IndirectOffsetOnAxis(ap=p[:, j:j + 1], axis=0),
                                             in_=h2all[:, j, :], in_offset=None).then_inc(S["scat"], 16)

        def counts():
            @step("dve")
            def _(e):
                e.tensor_copy(nf[:, :], csum[:, :]).then_inc(S["nc"], 1)

            @step("pe")
            def _(e):
                w(e, "nc", 1)
                e.matmul(tp[1][:, 0:E], ones[:, :], nf[:, :], start=True, stop=True).then_inc(S["nc"], 1)

            @step("dve")
            def _(e):
                w(e, "nc", 2)
                link(e, e.tensor_copy(nf[:, :], tp[1][:, 0:E]))
                link(e, e.tensor_tensor(ncmp[:, :, :], nf[:, :].unsqueeze(2).to_broadcast([128, E, 7]), thr,
                                        ALU.is_gt))
                link(e, e.tensor_reduce(kf[:, :], ncmp[:, :, :], AX, ALU.add))
                e.tensor_scalar(kint[:, :], kf[:, :], 1.0, None, ALU.add).then_inc(S["kr"], 1)
                link(e, e.tensor_tensor_scan(yoff[:, 0, :], ones[:, 0:E], nf[:, :], 0.0, ALU.mult, ALU.add))
                link(e, e.tensor_tensor(yoff[:, 1, :], yoff[:, 0, :], nf[:, :], ALU.subtract))
                e.tensor_copy(yoint[:, :], yoff[:, 1, :]).then_inc(S["kr"], 1)
                e.tensor_scalar(nmint[:, :], nf[:, :], -float(T), 0.0, ALU.add, ALU.max).then_inc(S["kr"], 1)
                w(e, "kr", 3)

        def weights():
            @step("dve")
            def _(e):
                link(e, e.tensor_tensor(yoff[:, 2, :], yoff[:, 1, :], ebase[:, 0, :], ALU.subtract))
                for q in range(2):
                    link(e, e.tensor_tensor(exd, sel[:, q, :, :], bc(yoff[:, 2, :], 4 * NG), ALU.mult))
                    link(e, e.tensor_reduce(exd2, exd, AX, ALU.add))
                    link(e, e.tensor_copy(cw[:, 0, :], pos[:, q, :]))
                    link(e, e.tensor_tensor(cw[:, 0, :], cw[:, 0, :], exd2, ALU.add))
                    link(e, e.tensor_copy(posy[:, q, :], cw[:, 0, :]))
                link(e, e.tensor_tensor(exd2, mx2[:, :], mx1[:, :], ALU.subtract))
                e.tensor_tensor(exd, Lall[:, :, :], mx1[:, :].unsqueeze(2).to_broadcast([128, 4 * NG, E]),
                                ALU.subtract).then_inc(S["e1"], 1)

            @step("act")
            def _(e):
                w(e, "e1", 1)
                link(e, e.activation(exd, exd, ACT.Exp), "ach")
                e.activation(exd2, exd2, ACT.Exp).then_inc(S["e2"], 1)

            @step("dve")
            def _(e):
                w(e, "e2", 1)
                link(e, e.tensor_reduce(cw[:, 0, :], exd, AX, ALU.add))
                link(e, e.reciprocal(cw[:, 1, :], cw[:, 0, :]))
                link(e, e.tensor_tensor(cw[:, 2, :], exd2, cw[:, 1, :], ALU.mult))
                link(e, e.scalar_tensor_tensor(cw[:, 0, :], cw[:, 1, :], 1e-8, cw[:, 2, :], ALU.add, ALU.add))
                link(e, e.reciprocal(cw[:, 3, :], cw[:, 0, :]))
                link(e, e.tensor_tensor(cw[:, 0, :], cw[:, 1, :], cw[:, 3, :], ALU.mult))
                e.tensor_tensor(cw[:, 1, :], cw[:, 2, :], cw[:, 3, :], ALU.mult).then_inc(S["cw"], 1)

        def split_expert(hi, lo, n, after=None):
            @step(hi)
            def _(e):
                if after:
                    w(e, *after)
                w(e, "raw", 32 * (n + 1))
                for q in range(2):
                    r = slice(q * 2048, (q + 1) * 2048)
                    if hi == "act":
                        e.activation(SH[n % 2][:, r], wraw[:, r], ACT.Copy).then_inc(S["sph"], 1)
                    else:
                        e.tensor_copy(SH[n % 2][:, r], wraw[:, r]).then_inc(S["sph"], 1)

            @step(lo)
            def _(e):
                for q in range(2):
                    r = slice(q * 2048, (q + 1) * 2048)
                    w(e, "sph", 2 * n + q + 1)
                    e.tensor_tensor(SL[n % 2][:, r], wraw[:, r], SH[n % 2][:, r].bitcast(F32), ALU.subtract)\
                        .then_inc(S["spl"], 1)

        def trips(e, n):
            return e.value_load(kint[0:1, n:n + 1], min_val=1, max_val=CAP // T)

        def pe_experts(e):
            rl = {k: e.alloc_register("pe_" + k) for k in ("g", "hlo", "yev", "xin", "fl")}
            for r in rl.values():
                e.reg_mov(r, 0)

            def due(name, by):
                e.reg_add(rl[name], rl[name], by)
                e.wait_ge(S[name], rl[name])

            def turn():
                due("xin", 16)
                for k in range(2):
                    for j in range(4):
                        i = e.transpose(tp[k][:, j * 128:(j + 1) * 128], xin[:, j, k * 128:(k + 1) * 128],
                                        ident[:, :])
                    i.then_inc(S["tp2"], 1)

            e.reg_mov(rl["hlo"], 2)
            e.sem_inc(S["l2"], NF)
            w(e, "kr", 3)
            turn()
            for n in range(E):
                s = n % 2
                w1h, w1l = (t[s][:, 0:2048].rearrange("p (c n) -> p c n", c=2) for t in (SH, SL))
                w2h, w2l = (t[s][:, 2048:4096].rearrange("p (c n) -> p c n", c=NF) for t in (SH, SL))
                k_n = trips(e, n)
                w(e, "spl", 2 * (n + 1))

                def layer1(f):
                    due("g", 1)
                    for k in range(2):
                        for t, (a, b) in enumerate(((w1h, fh), (w1h, fl), (w1l, fh))):
                            i = e.matmul(mm[f % 4][:, :], a[:, k, f * 128:(f + 1) * 128], b[:, k, :],
                                         start=(k == 0 and t == 0), stop=(k == 1 and t == 2))
                    i.then_inc(S["l1"], 1)

                def layer2(f):
                    if f == 0:
                        due("yev", 1)
                    due("hlo", 1)
                    for j in range(4):
                        o = yb[j // 2][:, (j % 2) * D:(j % 2 + 1) * D]
                        for t, (a, b) in enumerate(((hh, w2h), (hh, w2l), (hl, w2h))):
                            i = e.matmul(o, a[:, f, j * 128:(j + 1) * 128], b[:, f, :],
                                         start=(f == 0 and j % 2 == 0 and t == 0), stop=(f == NF - 1 and t == 2),
                                         skip_group_check=True)
                    i.then_inc(S["l2"], 1)

                with e.Fori(0, k_n):
                    due("fl", 2)
                    for f in range(NF):
                        layer1(f)
                        if f >= 2:
                            layer2(f - 2)
                    turn()
                    layer2(NF - 2)
                    layer2(NF - 1)

        def act_experts(e):
            rl = {k: e.alloc_register("act_" + k) for k in ("l1", "hlo", "l2", "tp2")}
            for r in rl.values():
                e.reg_mov(r, 0)

            def due(name, by):
                e.reg_add(rl[name], rl[name], by)
                e.wait_ge(S[name], rl[name])

            def part():
                for k in range(2):
                    due("tp2", 1)
                    e.activation(fh[:, k, :], tp[k][:, :], ACT.Copy).then_inc(S["fh"], 1)

            e.reg_mov(rl["tp2"], 2)
            e.sem_inc(S["g"], 4)
            w(e, "kr", 3)
            part()
            w(e, "b1T", 1)
            for n in range(E):
                k_n = trips(e, n)
                with e.Fori(0, k_n):
                    for f in range(NF):
                        due("l1", 1)
                        due("hlo", 1)
                        due("l2", 1)
                        bias = b1T[:, n * NF + f:n * NF + f + 1]
                        e.activation(h32[:, f % 2, :], mm[f % 4][:, :], ACT.Gelu_apprx_tanh, bias=bias)
                        e.activation(hh[:, f, :], mm[f % 4][:, :], ACT.Gelu_apprx_tanh, bias=bias)\
                            .then_inc(S["g"], 1)
                    part()

        def dve_experts(e):
            rl = {k: e.alloc_register("dve_" + k) for k in ("g", "fh", "l2", "yf")}
            for r in rl.values():
                e.reg_mov(r, 0)
            e.reg_mov(rl["g"], 4)
            e.reg_mov(rl["l2"], NF)

            def due(name, by):
                e.reg_add(rl[name], rl[name], by)
                e.wait_ge(S[name], rl[name])

            def part():
                for k in range(2):
                    due("fh", 1)
                    e.tensor_tensor(fl[:, k, :], tp[k][:, :], fh[:, k, :].bitcast(F32), ALU.subtract)\
                        .then_inc(S["fl"], 1)

            e.sem_inc(S["hlo"], 2)
            e.sem_inc(S["yev"], 1)
            part()
            for n in range(E):
                k_n = trips(e, n)
                if n == 0:
                    w(e, "b2", 16)
                with e.Fori(0, k_n):
                    for f in range(NF):
                        due("g", 1)
                        e.tensor_tensor(hl[:, f, :], h32[:, f % 2, :], hh[:, f, :].bitcast(F32), ALU.subtract)\
                            .then_inc(S["hlo"], 1)
                    part()
                    due("l2", NF)
                    due("yf", 1)
                    for q in range(2):
                        i = e.tensor_tensor(ysb[:, 2 * q:2 * q + 2, :],
                                            yb[q][:, :].rearrange("p (j d) -> p j d", j=2), bc(b2b[:, n, :], 2),
                                            ALU.add)
                    i.then_inc(S["yev"], 1)

        def tile_start(e, r_at, r_pos, r_last, base, most):
            e.reg_alu(r_at, r_pos, r_last, ALU.min)
            e.reg_add(r_at, r_at, base)
            return e.snap(r_at, min_val=0, max_val=most)

        def sp_experts(e):
            r_pos, r_at, r_last, r_tp = (e.alloc_register("sp_" + k) for k in ("pos", "at", "last", "tp2"))
            w(e, "kr", 3)
            e.dma_start(b2b[:, :, :].rearrange("p e d -> p (e d)"),
                        b2.rearrange("e d -> (e d)").partition_broadcast(128)).then_inc(S["b2"], 16)
            w(e, "scat", 16 * 8 * NG)
            e.reg_mov(r_tp, 0)
            e.sem_inc(S["tp2"], 2)
            for n in range(E):
                if n + 1 < E:
                    w(e, "spl", 2 * (n + 1))
                    load_expert(e, n + 1)
                k_n = trips(e, n)
                e.reg_load(r_last, nmint[0:1, n:n + 1])
                e.reg_mov(r_pos, 0)
                with e.Fori(0, k_n):
                    e.reg_add(r_tp, r_tp, 2)
                    e.wait_ge(S["tp2"], r_tp)
                    at = tile_start(e, r_at, r_pos, r_last, n * CAP, (E - 1) * CAP + CAP - T)
                    e.dma_start(xin[:, :, :], Xd[bass.ds(at, T), :].rearrange("(j p) d -> p j d", p=128))\
                        .then_inc(S["xin"], 16)
                    e.reg_add(r_pos, r_pos, T)
            e.reg_add(r_tp, r_tp, 2)
            e.wait_ge(S["tp2"], r_tp)
            e.dma_start(xin[:, :, :], Xd[0:T, :].rearrange("(j p) d -> p j d", p=128)).then_inc(S["xin"], 16)

        def pool_experts(e):
            r_pos, r_at, r_last, r_off, r_ev, r_st = (e.alloc_register("pool_" + k)
                                                      for k in ("pos", "at", "last", "off", "yev", "yst"))
            e.sem_inc(S["yf"], 1)
            w(e, "kr", 3)
            e.reg_mov(r_ev, 1)
            e.reg_mov(r_st, 0)
            for n in range(E):
                for q in range(2 if n + 1 < E else 0):
                    r = slice(q * 2048, (q + 1) * 2048)
                    m = n + 1
                    w(e, "raw", 32 * (m + 1))
                    e.tensor_copy(SH[m % 2][:, r], wraw[:, r]).then_inc(S["sph"], 1)
                    w(e, "sph", 2 * m + q + 1)
                    e.tensor_tensor(SL[m % 2][:, r], wraw[:, r], SH[m % 2][:, r].bitcast(F32), ALU.subtract)\
                        .then_inc(S["spl"], 1)
                k_n = trips(e, n)
                e.reg_load(r_last, nmint[0:1, n:n + 1])
                e.reg_load(r_off, yoint[0:1, n:n + 1])
                e.reg_mov(r_pos, 0)
                with e.Fori(0, k_n):
                    e.reg_add(r_ev, r_ev, 1)
                    e.wait_ge(S["yev"], r_ev)
                    at = tile_start(e, r_at, r_pos, r_last, r_off, 2 * TOK)
                    e.dma_start(Yd[bass.ds(at, T), :].rearrange("(j p) d -> p j d", p=128), ysb[:, :, :])\
                        .then_inc(S["yst"], 16)
                    e.reg_add(r_pos, r_pos, T)
                    e.reg_add(r_st, r_st, 16)
                    e.wait_ge(S["yst"], r_st)
                    e.sem_inc(S["yf"], 1)
            e.sem_inc(S["fin"], 1)

        def load_x2(g):
            @step("sp")
            def _(e):
                if g == 0:
                    w(e, "fin", 1)
                    e.dma_start(gbb[:, :, :], modd[:, 5 * D:6 * D].partition_broadcast(128)).then_inc(S["gbb"], 16)
                    w(e, "x2w0", 16 * (NG // 2))
                    w(e, "x2w1", 16 * (NG // 2))
                w(e, "fo", g - 1)
                e.dma_start(x2r[:, g % 2, :, :], rows(x2d, g)).then_inc(S[f"xr{g % 2}"], 16)

        def combine(g):
            @step("pool")
            def _(e):
                w(e, "ft", g - 1)
                for j in range(4):
                    for p, buf in ((posy[:, 0, :], ga_), (posy[:, 1, :], gb_)):
                        e.indirect_dma_start(out=buf[:, g % 2, j, :], out_offset=None, in_=Yd,
                                             in_offset=bass.IndirectOffsetOnAxis(
                                                 ap=p[:, 4 * g + j:4 * g + j + 1], axis=0))\
                            .then_inc(S[f"ga{g % 2}"], 16)

            @step("act")
            def _(e):
                w(e, f"ga{g % 2}", 128 * (g // 2 + 1))
                w(e, "cw", 1)
                for j in range(4):
                    i = e.activation(ga_[:, g % 2, j, :], ga_[:, g % 2, j, :], ACT.Copy,
                                     scale=cw[:, 0, 4 * g + j:4 * g + j + 1])
                i.then_inc(S["gs"], 1)

            @step("dve")
            def _(e):
                w(e, "gs", g + 1)
                w(e, "gbb", 16)
                w(e, f"ou{g % 2}", 16 * (g // 2))
                o = ores[:, g % 2, :, :]
                for j in range(4):
                    i = e.scalar_tensor_tensor(ores[:, g % 2, j, :], gb_[:, g % 2, j, :],
                                               cw[:, 1, 4 * g + j:4 * g + j + 1], ga_[:, g % 2, j, :],
                                               ALU.mult, ALU.add)
                i.then_inc(S["ft"], 1)
                w(e, "ft", g + 1)
                link(e, e.tensor_tensor(o, o, bc(gbb[:, g // 2, :], 4), ALU.mult))
                w(e, f"xr{g % 2}", 16 * (g // 2 + 1))
                e.tensor_tensor(o, o, x2r[:, g % 2, :, :], ALU.add).then_inc(S["fo"], 1)

            @step("sp")
            def _(e):
                w(e, "fo", g + 1)
                e.dma_start(rows(out_rows, g), ores[:, g % 2, :, :]).then_inc(S[f"ou{g % 2}"], 16)

        setup()
        ln1(0)
        xt(0)

        def has(g):
            return 0 <= g < NG

        for g in range(NG + 2):
            if has(g + 1):
                ln1(g + 1)
            if has(g):
                main(g, 0)
            if has(g - 1):
                split_o(g - 1, 3)
                project(g - 1, 2)
            if has(g - 2):
                turn_h(g - 2)
            if has(g):
                main(g, 1)
                split_o(g, 0)
            if has(g - 1):
                project(g - 1, 3)
                post(g - 1)
            if has(g - 2):
                logits(g - 2)
            if has(g):
                main(g, 2)
                split_o(g, 1)
                project(g, 0)
            if has(g - 1):
                ln2(g - 1)
            if has(g - 2):
                rank(g - 2)
                scatter(g - 2)
            if has(g):
                main(g, 3)
                split_o(g, 2)
            if has(g + 1):
                xt(g + 1)
            if has(g):
                project(g, 1)
        split_expert("act", "dve", 0, after=("mm", 16 * NG))
        counts()
        weights()

        @step("act")
        def _(e):
            w(e, "kr", 3)
            e.activation(b1T[:, :], vT[:, 0:64], ACT.Copy).then_inc(S["b1T"], 1)

        for name, fn in (("sp", sp_experts), ("pool", pool_experts), ("act", act_experts), ("pe", pe_experts),
                         ("dve", dve_experts)):
            steps.append((name, fn))
        load_x2(0)
        load_x2(1)
        for g in range(NG):
            combine(g)
            if g + 2 < NG:
                load_x2(g + 2)

        @step("sp")
        def _(e):
            w(e, "ou0", 16 * (NG // 2))
            w(e, "ou1", 16 * (NG // 2))

        def emit(name, e):
            for engine, fn in steps:
                if engine == name:
                    fn(e)

        block = ctx.enter_context(nc.Block())

        @block.sync
        def _(e):
            emit("sp", e)

        @block.gpsimd
        def _(e):
            emit("pool", e)

        @block.scalar
        def _(e):
            emit("act", e)

        @block.tensor
        def _(e):
            emit("pe", e)

        @block.vector
        def _(e):
            emit("dve", e)


INPUTS = ("L0_attn_x", "L0_attn_rms_scale", "L0_attn_split_scale", "L0_attn_W_K", "L0_attn_W_ugg", "L0_attn_W_out",
          "L0_ffn_Wg", "L0_ffn_bg", "L0_ffn_W1", "L0_ffn_b1", "L0_ffn_W2", "L0_ffn_b2", "L0_c", "L0_wmod")


def kernel(**inputs):
    import numpy as np
    import concourse.bacc as bacc
    from concourse.bass_utils import run_bass_kernel_spmd as run

    nc = bacc.Bacc("TRN2", target_bir_lowering=False, num_devices=1)
    arrays, args = {}, []
    for name in INPUTS:
        a = np.ascontiguousarray(inputs[name])
        arrays["in_" + name] = a
        args.append(nc.dram_tensor("in_" + name, a.shape, mybir.dt.from_np(a.dtype), kind="ExternalInput").ap())
    out = nc.dram_tensor("out_x", (NB, TOK // NB, D), F32, kind="ExternalOutput").ap()
    build(nc, *args, out)
    r = run(nc, [arrays], core_ids=[0])
    return r.results[0]["out_x"]
```

```python
from contextlib import ExitStack

import concourse.bass as bass
from concourse import mybir

F32 = mybir.dt.float32
F32R = mybir.dt.float32r
BF16 = mybir.dt.bfloat16
I32 = mybir.dt.int32
ALU = mybir.AluOpType
ACT = mybir.ActivationFunctionType
AX = mybir.AxisListType.X

D = 256
H = 512
E = 8
FF = 1024
NF = FF // 128
T = 512
TE = 256
MW = 8
DW = D + MW
NG = 8
NB = 4
TOK = NG * T
CAP = TOK
MAGIC = 0x5F3759DF


def build(nc, x, rms, split, W_K, W_ugg, W_out, Wg, bg, W1, b1, W2, b2, c, wmod, out):
    x_rows = x.rearrange("b s d -> (b s) d")
    out_rows = out.rearrange("b s d -> (b s) d")
    Xd = nc.dram_tensor("disp_x", (E * CAP + E * 256, DW), F32, kind="Internal").ap()
    Xm = Xd.rearrange("r (q c) -> (r q) c", c=MW)
    modd = nc.dram_tensor("mod_rows", (NB, 6 * D), F32, kind="Internal").ap()

    def rows(t, g):
        return t[g * T:(g + 1) * T, :].rearrange("(j p) d -> p j d", p=128)

    with ExitStack() as ctx:
        def sem(name):
            return ctx.enter_context(nc.semaphore(name))

        def sb(stack, name, shape, dt=F32):
            return stack.enter_context(nc.sbuf_tensor(name, shape, dt))

        h2all = sb(ctx, "h2all", [128, 4 * NG, DW])
        wraw0 = sb(ctx, "wraw", [128, 4096])
        mb = sb(ctx, "mb", [128, 3, 6 * D])
        x2b = sb(ctx, "x2b", [128, 2, 4, D])
        ident = sb(ctx, "ident", [128, 128])
        upper = sb(ctx, "upper", [128, 128], BF16)
        ones = sb(ctx, "ones", [128, 128], BF16)
        zcol = sb(ctx, "zcol", [128, 1])
        vrow = sb(ctx, "vrow", [76, 128])
        vT = sb(ctx, "vT", [128, 76])
        sv = sb(ctx, "sv", [128, 2])
        sgc = sb(ctx, "sgc", [128, 8])
        scT = sb(ctx, "scT", [128, 2, NB])
        wg = sb(ctx, "wg", [128, 2, E])
        bgb = sb(ctx, "bgb", [128, E])
        ioi = sb(ctx, "ioi", [128, 210], I32)
        iof = sb(ctx, "iof", [128, 210])
        bst = sb(ctx, "bst", [128, 2, 4, 6])
        mv = sb(ctx, "mv", [128, 2, 4, 2])
        nt = sb(ctx, "nt", [128, 8, 4])
        rsn = sb(ctx, "rsn", [128, 2, 2, 4])
        ss = sb(ctx, "ss", [128, 2, 4])
        rin = sb(ctx, "rin", [128, 2, 4])
        rsn2 = sb(ctx, "rsn2", [128, 2, 2, 4])
        Lg = sb(ctx, "Lg", [128, 4, E])
        mx1 = sb(ctx, "mx1", [128, 4])
        mx2 = sb(ctx, "mx2", [128, 4])
        rt = sb(ctx, "rt", [128, 4, 4, E])
        rmin = sb(ctx, "rmin", [128, 4])
        sel = sb(ctx, "sel", [128, 2, 4, E])
        selb = sb(ctx, "selb", [128, 4, E], BF16)
        csum = sb(ctx, "csum", [128, E], BF16)
        pos = sb(ctx, "pos", [128, 2, 4 * NG], I32)
        exw = sb(ctx, "exw", [128, 4, E + 1])
        sgw = sb(ctx, "sgw", [128, 4, E + 1])
        wsum = sb(ctx, "wsum", [128, 2, 4])
        prem = sb(ctx, "prem", [128, 2, MW])
        prex = sb(ctx, "prex", [128, 4, 2, E])
        prei = sb(ctx, "prei", [128, 2, E], I32)
        nf = sb(ctx, "nf", [128, 2, E])
        few = sb(ctx, "few", [128, 1], I32)
        gl = sb(ctx, "gl", [128, 1])
        lateint = sb(ctx, "lateint", [1, 1], I32)
        ncmp = sb(ctx, "ncmp", [128, 2, E, 14])
        kf2 = sb(ctx, "kf2", [128, 2, E])
        kpk = sb(ctx, "kpk", [128, 2], I32)
        kf = sb(ctx, "kf", [128, E])
        nmint = sb(ctx, "nmint", [128, E], I32)

        tp = [ctx.enter_context(nc.psum_tensor(f"tp{i}", [128, 512], F32)) for i in range(2)]
        mm = [ctx.enter_context(nc.psum_tensor(f"mm{i}", [128, 512], F32)) for i in range(4)]
        yb = [ctx.enter_context(nc.psum_tensor(f"yb{i}", [128, 512], F32)) for i in range(2)]

        with ExitStack() as p1:
            WH = sb(p1, "WH", [128, 2, 2048], F32R)
            WL = sb(p1, "WL", [128, 2, 2048], F32R)
            WOH = sb(p1, "WOH", [128, 4, D], F32R)
            WOL = sb(p1, "WOL", [128, 4, D], F32R)
            xb = sb(p1, "xb", [128, 3, 4, D])
            hb = sb(p1, "hb", [128, 3, 4, D])
            xnb = sb(p1, "xnb", [128, 4, D])
            xh = sb(p1, "xh", [128, 2, 2, T], F32R)
            xl = sb(p1, "xl", [128, 2, 2, T], F32R)
            kb = sb(p1, "kb", [128, 4, T + 1])
            sgi = sb(p1, "sgi", [128, 2, T])
            sgo = sb(p1, "sgo", [128, 2, T])
            ub = sb(p1, "ub", [128, T])
            ob = sb(p1, "ob", [128, T])
            cy = sb(p1, "cy", [128, 4])
            og = sb(p1, "og", [128, 2, T])
            oh = sb(p1, "oh", [128, 3, T], F32R)
            ol = sb(p1, "ol", [128, 3, T], F32R)
            h2T = sb(p1, "h2T", [128, 2, T])
        with ExitStack() as p2:
            SH = [None, None]
            SL = [None, None]
            for i in range(2):
                SH[i] = sb(p2, f"SH{i}", [128, 4096], F32R)
                SL[i] = sb(p2, f"SL{i}", [128, 4096], F32R)
            xin = sb(p2, "xin", [128, 2, DW])
            xm = sb(p2, "xm", [128, 2, MW])
            tokb = sb(p2, "tokb", [128, 2], I32)
            wsl = sb(p2, "wsl", [128, 3, 2, 2])
            wB = sb(p2, "wB", [128, 2])
            nom = sb(p2, "nom", [128, 2])
            gbr = sb(p2, "gbr", [128, 2, D])
            fh = sb(p2, "fh", [128, 2, TE], F32R)
            fl = sb(p2, "fl", [128, 2, TE], F32R)
            h32 = sb(p2, "h32", [128, 2, TE])
            hh = sb(p2, "hh", [128, NF, TE], F32R)
            hl = sb(p2, "hl", [128, NF, TE], F32R)
            ysb = sb(p2, "ysb", [128, 2, D])
            b1T = sb(p2, "b1T", [128, E * NF])
        x2f = x2b[:, :, :, :].rearrange("p a j d -> p (a j d)")
        b2b = x2f.rearrange("p (e d) -> p e d", e=E)
        modr = x2f[0:NB, 0:6 * D]
        mtmp = x2f[0:NB, 6 * D:8 * D].rearrange("p (a d) -> p a d", a=2)
        h2f = h2all[:, :, :].rearrange("p a d -> p (a d)")
        wmod_sb = h2f[:, 0:12 * D].rearrange("p (c n) -> p c n", c=2)
        wo_raw = h2f[:, 12 * D:16 * D].rearrange("p (c n) -> p c n", c=4)
        zfill = h2all[:, 31, :]
        wraw = [wraw0[:, :], h2f[:, 0:4096]]
        wat = wraw[0].rearrange("p (c n) -> p c n", c=2)
        em8 = iof[:, 0:32].rearrange("p (j e) -> p j e", j=4)
        ebase = iof[:, 32:64].rearrange("p (j e) -> p j e", j=4)
        thr = iof[:, 64:176].rearrange("p (e m) -> p e m", e=E)
        tq = iof[:, 176:178]
        nom0 = iof[:, 178:180]
        p32 = iof[:, 196:204].rearrange("p (h i) -> p h i", h=2)
        dump = iof[:, 180:196].rearrange("p (j e) -> p j e", j=2)

        names = ("xa", "xb_", "xc", "wa", "wa2", "wo", "wmod", "wmod2", "vec", "gat", "b2", "cst", "iota", "vT", "vTc", "sgc", "scT", "sv",
                 "mod", "md", "modc", "modr", "modw", "mb0", "mb1", "mb2", "zs", "zf", "wh", "wl", "woh", "wol", "b1T",
                 "s1", "z", "h", "sq", "r", "xn", "xt", "xh", "xl", "bas", "mm", "sg", "k", "so", "u", "w", "sc",
                 "og", "oh", "ol", "ol_", "cy", "y", "t1", "x2", "x2w0", "x2w1", "s2", "z2", "z2_", "h2", "h2_", "ht", "he", "lg", "m",
                 "la", "rk", "rr", "pos", "scat0", "scat1", "scat2", "cs", "late", "nc", "kr", "ch", "ch2", "ach", "pch", "e1", "e2", "cw", "prei", "pre0", "pre1", "few", "filled", "met", "ma", "gg", "ch3", "tick_pool", "tick_sp", "raw0", "raw1", "sph", "sph2", "spl", "spl2",
                 "xin", "tp2", "fh", "fl", "l1", "g", "hlo", "l2", "yev", "yst", "yf", "fin",
                 )
        S = {n: sem("s_" + n) for n in names}

        def w(eng, name, n):
            if n > 0:
                eng.wait_ge(S[name], n)

        def bc(ap, j):
            return ap.unsqueeze(1).to_broadcast([128, j, ap.shape[-1]])

        steps = []

        def step(engine):
            def add(fn):
                steps.append((engine, fn))
                return fn
            return add

        count = {"ch": 0, "ch2": 0, "ch3": 0, "ach": 0, "pch": 0}

        def link(eng, ins, name="ch"):
            count[name] += 1
            ins.then_inc(S[name], 1)
            eng.wait_ge(S[name], count[name])

        def lk(eng, ins, name="ch"):
            count[name] += 1
            n = count[name]
            ins.then_inc(S[name], 1)
            yield
            eng.wait_ge(S[name], n)

        def weave(*chains):
            live = list(chains)
            while live:
                for c_ in list(live):
                    try:
                        next(c_)
                    except StopIteration:
                        live.remove(c_)

        def mod(b, n):
            return mb[:, b % 3, n * D:(n + 1) * D]

        def rsqrt(e, v, y, a):
            yield from lk(e, e.tensor_scalar(a.bitcast(I32), v.bitcast(I32), 1, None, ALU.logical_shift_right))
            yield from lk(e, e.tensor_scalar(y.bitcast(I32), a.bitcast(I32), -1, MAGIC, ALU.mult, ALU.add))
            for _ in range(3):
                yield from lk(e, e.tensor_tensor(a, y, y, ALU.mult))
                yield from lk(e, e.scalar_tensor_tensor(a, a, -0.5, v, ALU.mult, ALU.mult))
                yield from lk(e, e.scalar_tensor_tensor(y, a, 1.5, y, ALU.add, ALU.mult))

        def moments(e, src, q, y, early):
            for j in range(4):
                i = e.bn_stats(bst[:, q, j, :], src[:, j, :])
            yield from lk(e, i)
            for j in range(4):
                i = e.bn_aggr(mv[:, q, j, :], bst[:, q, j, :])
            yield from lk(e, i)
            v, a = nt[:, 2 * q, :], nt[:, 2 * q + 1, :]
            yield from lk(e, e.tensor_scalar(v, mv[:, q, :, 1], 1e-5, None, ALU.add))
            w(e, *early)
            yield from rsqrt(e, v, y[:, 0, :], a)
            return e.scalar_tensor_tensor(y[:, 1, :], mv[:, q, :, 0], -1.0, y[:, 0, :], ALU.mult, ALU.mult)

        def setup():
            @step("sp")
            def _(e):
                e.dma_start(xb[:, 0, :, :], rows(x_rows, 0)).then_inc(S["xa"], 16)
                for t, (src, n) in enumerate(((b1.rearrange("e (f p) -> (e f) p", p=128), 64),
                                              (rms.rearrange("(c p) -> c p", p=128), 2),
                                              (split.rearrange("(c p) -> c p", p=128), 2),
                                              (c.rearrange("b (c p) -> (b c) p", p=128), 8))):
                    r0 = (0, 64, 66, 68)[t]
                    e.dma_start(vrow[r0:r0 + n, :], src).then_inc(S["vec"], 16)
                e.dma_start(wmod_sb[:, :, 0:512], wmod[:, 0:512].rearrange("(c p) n -> p c n", p=128))\
                    .then_inc(S["wmod"], 16)
                e.dma_start(wat[:, :, 0:H], W_K.rearrange("(c p) n -> p c n", p=128)).then_inc(S["wa"], 16)
                e.dma_start(wmod_sb[:, :, 512:1536], wmod[:, 512:1536].rearrange("(c p) n -> p c n", p=128))\
                    .then_inc(S["wmod2"], 16)
                e.dma_start(wat[:, :, H:4 * H], W_ugg.rearrange("(c p) n -> p c n", p=128)).then_inc(S["wa2"], 16)
                e.dma_start(wo_raw, W_out.rearrange("(c p) n -> p c n", p=128)).then_inc(S["wo"], 16)
                e.dma_start(wg[:, :, :], Wg.rearrange("(c p) n -> p c n", p=128)).then_inc(S["gat"], 16)
                e.dma_start(bgb[:, :], bg.partition_broadcast(128)).then_inc(S["gat"], 16)
                e.dma_start(xb[:, 1, :, :], rows(x_rows, 1)).then_inc(S["xb_"], 16)
                e.dma_start(xb[:, 2, :, :], rows(x_rows, 2)).then_inc(S["xc"], 16)
                w(e, "modr", 1)
                e.dma_start(modd, modr).then_inc(S["modw"], 16)
                w(e, "modw", 16)
                e.dma_start(mb[:, 0, 2 * D:6 * D], modd[0, 2 * D:6 * D].partition_broadcast(128))\
                    .then_inc(S["mb0"], 16)
                for b in range(1, 3):
                    e.dma_start(mb[:, b, :], modd[b, :].partition_broadcast(128)).then_inc(S[f"mb{b}"], 16)
                w(e, "zs", 1)
                for n in range(E):
                    e.dma_start(Xd[n * CAP:n * CAP + 128, :], zfill).then_inc(S["zf"], 16)
                w(e, "wl", 4)
                load_expert(e, 0)

            @step("pool")
            def _(e):
                e.memset(ident[:, :], 0.0).then_inc(S["cst"], 1)
                e.memset(upper[:, :], 1.0).then_inc(S["cst"], 1)
                e.memset(ones[:, :], 1.0).then_inc(S["cst"], 1)
                e.memset(zcol[:, :], 0.0).then_inc(S["cst"], 1)
                e.wait_ge(S["cst"], 4)
                e.affine_select(out=ident[:, :], in_=ident[:, :], compare_op=ALU.not_equal, fill=1.0, base=0,
                                pattern=[[-1, 128]], channel_multiplier=1).then_inc(S["cst"], 1)
                e.affine_select(out=upper[:, :], in_=upper[:, :], compare_op=ALU.is_gt, fill=0.0, base=0,
                                pattern=[[1, 128]], channel_multiplier=-1).then_inc(S["cst"], 1)
                e.memset(csum[:, :], 0.0).then_inc(S["cst"], 1)
                e.memset(zfill, 0.0).then_inc(S["zs"], 1)
                e.iota(ioi[:, 0:32].rearrange("p (j e) -> p j e", j=4), [[0, 4], [1, E]], base=-8,
                       channel_multiplier=0).then_inc(S["iota"], 1)
                e.iota(ioi[:, 32:64].rearrange("p (j e) -> p j e", j=4), [[0, 4], [CAP, E]], base=0,
                       channel_multiplier=0).then_inc(S["iota"], 1)
                e.iota(ioi[:, 64:176].rearrange("p (e m) -> p e m", e=E), [[0, E], [TE, 14]], base=2 * TE,
                       channel_multiplier=0).then_inc(S["iota"], 1)
                e.iota(ioi[:, 176:178], [[128, 2]], base=-127, channel_multiplier=1).then_inc(S["iota"], 1)
                e.iota(ioi[:, 180:196].rearrange("p (j e) -> p j e", j=2), [[128, 2], [256, E]], base=E * CAP,
                       channel_multiplier=1).then_inc(S["iota"], 1)
                for i in range(E // 2):
                    e.memset(p32[:, :, i], float(32 ** i)).then_inc(S["iota"], 1)
                e.iota(ioi[:, 178:180], [[128, 2]], base=0, channel_multiplier=0).then_inc(S["iota"], 1)
                e.memset(prem[:, :, :], 0.0).then_inc(S["met"], 1)
                w(e, "met", 1)
                e.memset(prem[:, :, 2:4], -1.0).then_inc(S["met"], 1)
                e.iota(prem[:, :, 4].bitcast(I32), [[128, 2]], base=0, channel_multiplier=1).then_inc(S["met"], 1)
                e.iota(prem[:, :, 5].bitcast(I32), [[0, 2]], base=5, channel_multiplier=0).then_inc(S["met"], 1)

            @step("pe")
            def _(e):
                w(e, "cst", 6)
                w(e, "vec", 64)
                e.transpose(tp[0][:, 0:76], vrow[:, :], ident[0:76, 0:76]).then_inc(S["vT"], 1)
                w(e, "scT", 1)
                w(e, "wmod", 16)
                for to, c0 in ((mm[3], D), (yb[0], 0)):
                    for k in range(2):
                        i = e.matmul(to[:, 0:D], scT[:, k, 0:1].to_broadcast([128, 128]), wmod_sb[:, k, c0:c0 + D],
                                     start=(k == 0), stop=(k == 1))
                    i.then_inc(S["mod"], 1)
                for n in range(3):
                    if n == 1:
                        w(e, "wmod2", 16)
                    for k in range(2):
                        i = e.matmul(mm[n][0:NB, :], scT[:, k, :], wmod_sb[:, k, n * 512:(n + 1) * 512],
                                     start=(k == 0), stop=(k == 1))
                    i.then_inc(S["mod"], 1)

            @step("act")
            def _(e):
                w(e, "cst", 4)
                e.activation(gl[:, :], zcol[:, :], ACT.Sigmoid)
                w(e, "vT", 1)
                e.activation(vT[:, :], tp[0][:, 0:76], ACT.Copy).then_inc(S["vTc"], 1)
                w(e, "vTc", 1)
                e.activation(sgc[:, :], vT[:, 68:76], ACT.Sigmoid).then_inc(S["sgc"], 1)

            @step("pool")
            def _(e):
                w(e, "vTc", 1)
                e.tensor_tensor(sv[:, :], vT[:, 64:66], vT[:, 66:68], ALU.mult).then_inc(S["sv"], 1)
                w(e, "sgc", 1)
                e.tensor_tensor(scT[:, :, :].rearrange("p c b -> p b c"),
                                vT[:, 68:76].rearrange("p (b c) -> p b c", b=NB),
                                sgc[:, :].rearrange("p (b c) -> p b c", b=NB), ALU.mult).then_inc(S["scT"], 1)
                w(e, "iota", 6 + E // 2)
                e.tensor_copy(iof[:, 0:196], ioi[:, 0:196]).then_inc(S["iota"], 1)

        def weights_hi(part, k):
            cols = slice(0, H) if part == 0 else slice(H, 4 * H)

            @step("act")
            def _(e):
                w(e, ("wa", "wa2")[part], 16)
                w(e, "sv", 1)
                e.activation(WH[:, k, cols], wat[:, k, cols], ACT.Copy, scale=sv[:, k:k + 1]).then_inc(S["wh"], 1)

        def weights_lo(part, k):
            cols = slice(0, H) if part == 0 else slice(H, 4 * H)

            @step("dve")
            def _(e):
                w(e, "wh", 2 * part + k + 1)
                e.scalar_tensor_tensor(WL[:, k, cols], wat[:, k, cols], sv[:, k:k + 1], WH[:, k, cols].bitcast(F32),
                                       ALU.mult, ALU.subtract).then_inc(S["wl"], 1)

        def weights_out():
            @step("act")
            def _(e):
                w(e, "wo", 16)
                e.activation(WOH[:, :, :], wo_raw, ACT.Copy).then_inc(S["woh"], 1)

            @step("dve")
            def _(e):
                w(e, "woh", 1)
                e.tensor_tensor(WOL[:, :, :], wo_raw, WOH[:, :, :].bitcast(F32), ALU.subtract).then_inc(S["wol"], 1)

        def mod_first():
            @step("dve")
            def _(e):
                w(e, "mod", 1)
                e.tensor_scalar(mb[:, 0, D:2 * D], mm[3][:, 0:D], 1.0, None, ALU.add).then_inc(S["md"], 1)
                w(e, "mod", 2)
                e.tensor_copy(mb[:, 0, 0:D], yb[0][:, 0:D]).then_inc(S["md"], 1)

        def mod_rows(n):
            @step("act")
            def _(e):
                w(e, "mod", n + 3)
                e.activation(modr[:, n * 512:(n + 1) * 512], mm[n][0:NB, :], ACT.Copy).then_inc(S["modc"], 1)

        def mod_guards():
            def one(e):
                return lambda n: e.tensor_scalar(modr[:, n * D:(n + 1) * D], modr[:, n * D:(n + 1) * D], 1.0, None,
                                                 ALU.add)

            def guard(e, n, t, name):
                m = modr[:, n * D:(n + 1) * D]
                yield from lk(e, e.scalar_tensor_tensor(t, m, -1.0, m, ALU.mult, ALU.max), name)
                yield from lk(e, e.tensor_scalar(m, m, 0.0, 2.0, ALU.is_ge, ALU.mult), name)
                yield from lk(e, e.tensor_scalar(t, t, 0.25, None, ALU.max), name)
                yield from lk(e, e.scalar_tensor_tensor(m, m, -1.0, t, ALU.add, ALU.mult), name)

            @step("dve")
            def _(e):
                w(e, "modc", 3)
                one(e)(1)
                one(e)(4)
                weave(guard(e, 2, mtmp[:, 0, :], "ch"), guard(e, 5, mtmp[:, 1, :], "ch2"))
                e.sem_inc(S["modr"], 1)

        def token_columns():
            @step("pool")
            def _(e):
                w(e, "wol", 1)
                w(e, "mod", 5)
                w(e, "zf", 16 * E)
                e.memset(h2all[:, :, D + 6:D + 8], 0.0).then_inc(S["met"], 1)
                e.iota(h2all[:, :, D + 4].bitcast(I32), [[128, 4 * NG]], base=0, channel_multiplier=1)\
                    .then_inc(S["met"], 1)
                e.iota(h2all[:, :, D + 5].rearrange("p (b t) -> p b t", b=NB).bitcast(I32), [[6, NB], [0, 8]], base=5,
                       channel_multiplier=0).then_inc(S["met"], 1)

        def load_expert(e, n):
            load_w1(e, n)
            load_w2(e, n)

        def load_w1(e, n):
            raw = wraw[n % 2]
            e.dma_start(raw[:, 0:2048].rearrange("p (c n) -> p c n", c=2),
                        W1[n].rearrange("(c p) n -> p c n", p=128)).then_inc(S[f"raw{n % 2}"], 16)

        def load_w2(e, n):
            raw = wraw[n % 2]
            e.dma_start(raw[:, 2048:4096].rearrange("p (c n) -> p c n", c=NF),
                        W2[n].rearrange("(c p) n -> p c n", p=128)).then_inc(S[f"raw{n % 2}"], 16)

        XS = ("xa", "xb_", "xc")

        def ln1_stats(e, g):
            w(e, XS[g % 3], 16 * (g // 3 + 1))
            i = yield from moments(e, xb[:, g % 3, :, :], 0, rsn[:, g % 2, :, :], ("z", g - 1))
            i.then_inc(S["s1"], 1)

        def ln1_h(g):
            b = g // 2

            @step("act")
            def _(e):
                w(e, "s1", g + 1)
                w(e, "t1", g - 2)
                for j in range(4):
                    i = e.activation(hb[:, g % 3, j, :], xb[:, g % 3, j, :], ACT.Identity,
                                     scale=rsn[:, g % 2, 0, j:j + 1], bias=rsn[:, g % 2, 1, j:j + 1])
                i.then_inc(S["z"], 1)

            @step("pool" if g else "dve")
            def _(e):
                if b == 0:
                    w(e, "md", 2)
                else:
                    w(e, f"mb{b % 3}", 16 * (b // 3 + 1))
                w(e, "z", g + 1)
                link(e, e.tensor_tensor(hb[:, g % 3, :, :], hb[:, g % 3, :, :], bc(mod(b, 1), 4), ALU.mult),
                     "pch" if g else "ch")
                e.tensor_tensor(hb[:, g % 3, :, :], hb[:, g % 3, :, :], bc(mod(b, 0), 4), ALU.add)\
                    .then_inc(S["h"], 1)

        def ln1_sq(g):
            @step("act")
            def _(e):
                w(e, "h", g + 1)
                w(e, "xt", 2 * g)
                w(e, "r", g - 1)
                for j in range(4):
                    i = e.activation(xnb[:, j, :], hb[:, g % 3, j, :], ACT.Square,
                                     accum_out=ss[:, g % 2, j:j + 1])
                i.then_inc(S["sq"], 1)

        def ln1_norm(e, g):
            w(e, "sq", g + 1)
            v, y, a, d = (nt[:, q, :] for q in range(4, 8))
            yield from lk(e, e.tensor_scalar(v, ss[:, g % 2, :], 1.0 / D, 1e-34, ALU.mult, ALU.max))
            yield from rsqrt(e, v, y, a)
            yield from lk(e, e.tensor_tensor(d, v, y, ALU.mult))
            yield from lk(e, e.tensor_scalar(d, d, 1e-8, None, ALU.add))
            w(e, "xn", g - 1)
            e.reciprocal(rin[:, g % 2, :], d).then_inc(S["r"], 1)

        def ln1_xn(g):
            @step("act")
            def _(e):
                w(e, "r", g + 1)
                for j in range(4):
                    i = e.activation(xnb[:, j, :], hb[:, g % 3, j, :], ACT.Copy, scale=rin[:, g % 2, j:j + 1])
                i.then_inc(S["xn"], 1)

        def xt(g):
            @step("pe")
            def _(e):
                w(e, "xn", g + 1)
                w(e, "vTc", 1)
                w(e, "xl", 2 * g)
                w(e, "rr", g - 3)
                for k in range(2):
                    for j in range(4):
                        i = e.transpose(tp[k][:, j * 128:(j + 1) * 128], xnb[:, j, k * 128:(k + 1) * 128],
                                        ident[:, :])
                    i.then_inc(S["xt"], 1)

            @step("act")
            def _(e):
                for k in range(2):
                    w(e, "xt", 2 * g + k + 1)
                    if g >= 2:
                        w(e, "mm", 16 * (g - 1))
                    e.activation(xh[:, g % 2, k, :], tp[k][:, :], ACT.Copy).then_inc(S["xh"], 1)

            @step("dve")
            def _(e):
                for k in range(2):
                    w(e, "xh", 2 * g + k + 1)
                    e.tensor_tensor(xl[:, g % 2, k, :], tp[k][:, :], xh[:, g % 2, k, :].bitcast(F32), ALU.subtract)\
                        .then_inc(S["xl"], 1)

        KINDS = (("sg", 2), ("u", 1), ("k", 0), ("so", 3))

        def main(g, hc, between=None):
            n = 4 * g + hc

            for part in range(2):
                @step("pe")
                def _(e, part=part):
                    w(e, "xl", 2 * g + 2)
                    w(e, "wl", 4)
                    if n == 0:
                        w(e, "modc", 3)
                        w(e, "md", 2)
                    for q in range(2 * part, 2 * part + 2):
                        ev, kind = KINDS[q]
                        w(e, ev, n)
                        c0 = kind * H + hc * 128
                        i = None
                        for k in range(2):
                            for t, (a, b) in enumerate(((WH, xh), (WH, xl), (WL, xh))):
                                i = e.matmul(mm[q][:, :], a[:, k, c0:c0 + 128], b[:, g % 2, k, :],
                                             start=(k == 0 and t == 0), stop=(k == 1 and t == 2))
                        i.then_inc(S["mm"], 1)
                if part == 0 and between:
                    between()

            @step("act")
            def _(e):
                w(e, "mm", 4 * n + 1)
                w(e, "u", n - 1)
                e.activation(sgi[:, n % 2, :], mm[0][:, :], ACT.Sigmoid).then_inc(S["sg"], 1)
                w(e, "sc", n - 3)
                w(e, "k", n - 3)
                link(e, e.activation(kb[:, hc, 0:1], kb[:, hc, T:T + 1] if g % 2 else zcol[:, :], ACT.Copy), "ach")
                w(e, "mm", 4 * n + 3)
                e.activation(kb[:, hc, 1:T + 1], mm[2][:, :], ACT.Sigmoid).then_inc(S["k"], 1)
                w(e, "mm", 4 * n + 4)
                w(e, "og", n - 1)
                e.activation(sgo[:, n % 2, :], mm[3][:, :], ACT.Sigmoid).then_inc(S["so"], 1)

            @step("dve")
            def _(e):
                w(e, "mm", 4 * n + 2)
                w(e, "sg", n + 1)
                e.tensor_tensor(ub[:, :], mm[1][:, :], sgi[:, n % 2, :], ALU.mult).then_inc(S["u"], 1)
                w(e, "k", n + 1)
                w(e, "u", n + 1)
                e.scalar_tensor_tensor(ub[:, :], kb[:, hc, 1:T + 1], 1.0, ub[:, :], ALU.subtract, ALU.mult)\
                    .then_inc(S["w"], 1)
                w(e, "w", n + 1)
                e.tensor_tensor_scan(ob[:, :], kb[:, hc, 0:T], ub[:, :],
                                     cy[:, hc:hc + 1] if g % 2 else 0.0, ALU.mult, ALU.add).then_inc(S["sc"], 1)
                w(e, "sc", n + 1)
                if g % 2 == 0:
                    link(e, e.tensor_copy(cy[:, hc:hc + 1], ob[:, T - 1:T]))

            @step("dve")
            def _(e):
                w(e, "so", n + 1)
                w(e, "ol", n - 1)
                e.tensor_tensor(og[:, n % 2, :], ob[:, :], sgo[:, n % 2, :], ALU.mult).then_inc(S["og"], 1)

        def split_o(g, hc):
            n = 4 * g + hc

            @step("act")
            def _(e):
                w(e, "og", n + 1)
                w(e, "y", n - 2)
                e.activation(oh[:, n % 3, :], og[:, n % 2, :], ACT.Copy).then_inc(S["oh"], 1)

            @step("pool" if n < 4 * NG - 1 else "dve")
            def _(e):
                w(e, "oh", n + 1)
                if n == 4 * NG - 1:
                    w(e, "y", n - 2)
                name = "ol" if n < 4 * NG - 1 else "ol_"
                e.tensor_tensor(ol[:, n % 3, :], og[:, n % 2, :], oh[:, n % 3, :].bitcast(F32), ALU.subtract)\
                    .then_inc(S[name], 1)

        def project(g, hc):
            n = 4 * g + hc

            @step("pe")
            def _(e):
                w(e, "ol", min(n + 1, 4 * NG - 1))
                if n == 4 * NG - 1:
                    w(e, "ol_", 1)
                w(e, "wol", 1)
                if hc == 0:
                    w(e, "t1", g)
                for j in range(4):
                    o = yb[j // 2][:, (j % 2) * D:(j % 2 + 1) * D]
                    for t, (a, b) in enumerate(((oh, WOH), (oh, WOL), (ol, WOH))):
                        i = e.matmul(o, a[:, n % 3, j * 128:(j + 1) * 128], b[:, hc, :],
                                     start=(hc == 0 and j % 2 == 0 and t == 0), stop=(hc == 3 and t == 2),
                                     skip_group_check=True)
                i.then_inc(S["y"], 1)

        def post(g):
            b = g // 2

            @step("dve")
            def _(e):
                w(e, "y", 4 * g + 4)
                w(e, "modw", 16)
                w(e, f"x2w{g % 2}", 16 * (g // 2))
                w(e, "z2", g - 1)
                for q in range(2):
                    i = e.tensor_tensor(x2b[:, g % 2, 2 * q:2 * q + 2, :], hb[:, g % 3, 2 * q:2 * q + 2, :],
                                        yb[q][:, :].rearrange("p (j d) -> p j d", j=2), ALU.subtract)
                i.then_inc(S["t1"], 1)

            @step("pool" if g < NG - 1 else "dve")
            def _(e):
                w(e, f"mb{b % 3}", 16 * (b // 3 + 1))
                w(e, "t1", g + 1)
                e.tensor_tensor(x2b[:, g % 2, :, :], x2b[:, g % 2, :, :], bc(mod(b, 2), 4), ALU.mult)\
                    .then_inc(S["bas"], 1)

        def add_x(g):
            @step("dve")
            def _(e):
                w(e, "bas", g + 1)
                e.tensor_tensor(x2b[:, g % 2, :, :], x2b[:, g % 2, :, :], xb[:, g % 3, :, :], ALU.add)\
                    .then_inc(S["x2"], 1)

            @step("sp")
            def _(e):
                w(e, "x2", g + 1)
                e.dma_start(rows(out_rows, g), x2b[:, g % 2, :, :]).then_inc(S[f"x2w{g % 2}"], 16)
                if g + 3 < NG:
                    e.dma_start(xb[:, g % 3, :, :], rows(x_rows, g + 3)).then_inc(S[XS[g % 3]], 16)

        def ln2_stats(e, g):
            w(e, "x2", g + 1)
            i = yield from moments(e, x2b[:, g % 2, :, :], 1, rsn2[:, g % 2, :, :], ("z2", g - 1))
            i.then_inc(S["s2"], 1)

        def ln2_h(g):
            b = g // 2

            last = g == NG - 1

            @step("dve" if last else "act")
            def _(e):
                w(e, "s2", g + 1)
                w(e, "wol", 1)
                w(e, "zf", 16 * E)
                for j in range(4):
                    y = h2all[:, 4 * g + j, 0:D], x2b[:, g % 2, j, :]
                    scale, bias = (rsn2[:, g % 2, q, j:j + 1] for q in range(2))
                    if last:
                        i = e.tensor_scalar(*y, scale, bias, ALU.mult, ALU.add)
                    else:
                        i = e.activation(*y, ACT.Identity, scale=scale, bias=bias)
                i.then_inc(S["z2_" if last else "z2"], 1)


            @step("dve" if last else "pool")
            def _(e):
                w(e, "z2_" if last else "z2", 1 if last else g + 1)
                hv = h2all[:, 4 * g:4 * g + 4, 0:D]
                link(e, e.tensor_tensor(hv, hv, bc(mod(b, 4), 4), ALU.mult), "ch" if last else "pch")
                e.tensor_tensor(hv, hv, bc(mod(b, 3), 4), ALU.add).then_inc(S["h2_" if last else "h2"], 1)

            @step("sp")
            def _(e):
                if g == 1:
                    w(e, "h2", g + 1)
                    e.dma_start(mb[:, 0, :], modd[3, :].partition_broadcast(128)).then_inc(S["mb0"], 16)

        def turn_h(g):
            @step("pe")
            def _(e):
                w(e, "h2", min(g + 1, NG - 1))
                w(e, "h2_", g - NG + 2)
                w(e, "xl", 2 * min(g + 4, NG))
                w(e, "rr", min(g, NG - 2))
                for k in range(2):
                    for j in range(4):
                        i = e.transpose(tp[k][:, j * 128:(j + 1) * 128],
                                        h2all[:, 4 * g + j, k * 128:(k + 1) * 128], ident[:, :])
                    i.then_inc(S["ht"], 1)

            @step("act")
            def _(e):
                w(e, "lg", g)
                for k in range(2):
                    w(e, "ht", 2 * g + k + 1)
                    e.activation(h2T[:, k, :], tp[k][:, :], ACT.Copy).then_inc(S["he"], 1)

        def at_logits(g):
            return tp[0][:, 0:4 * E] if g < NG - 2 else mm[2][:, 0:4 * E]

        def at_places(g):
            return tp[0][:, 128:160] if g < NG - 2 else mm[3][:, 0:4 * E]

        def logits(g):
            @step("pe")
            def _(e):
                w(e, "he", 2 * g + 2)
                w(e, "gat", 32)
                if g >= NG - 2:
                    w(e, "k", 4 * NG)
                    w(e, "m", g)
                o = at_logits(g)
                for j in range(4):
                    for k in range(2):
                        i = e.matmul(o[:, j * E:(j + 1) * E], h2T[:, k, j * 128:(j + 1) * 128], wg[:, k, :],
                                     start=(k == 0), stop=(k == 1))
                i.then_inc(S["lg"], 1)

        def top2(e, g):
            w(e, "lg", g + 1)
            m1, m2 = mx1[:, :], mx2[:, :]
            sel1, sel2 = (sel[:, q, :, :] for q in range(2))

            def wide(v):
                return v.unsqueeze(2).to_broadcast([128, 4, E])

            def first(src, mx, to):
                yield from lk(e, e.tensor_tensor(rt[:, 0, :, :], src, wide(mx), ALU.is_equal), "ch2")
                yield from lk(e, e.tensor_tensor(rt[:, 0, :, :], rt[:, 0, :, :], em8, ALU.mult), "ch2")
                yield from lk(e, e.tensor_reduce(rmin[:, :], rt[:, 0, :, :], AX, ALU.min), "ch2")
                yield from lk(e, e.tensor_tensor(to, em8, wide(rmin[:, :]), ALU.is_equal), "ch2")

            yield from lk(e, e.tensor_tensor(Lg[:, :, :], at_logits(g).rearrange("p (j e) -> p j e", j=4),
                                             bc(bgb[:, :], 4), ALU.add), "ch2")
            yield from lk(e, e.tensor_reduce(m1, Lg[:, :, :], AX, ALU.max), "ch2")
            yield from first(Lg[:, :, :], m1, sel1)
            yield from lk(e, e.scalar_tensor_tensor(rt[:, 1, :, :], sel1, -3e38, Lg[:, :, :], ALU.mult, ALU.add), "ch2")
            yield from lk(e, e.tensor_reduce(m2, rt[:, 1, :, :], AX, ALU.max), "ch2")
            yield from first(rt[:, 1, :, :], m2, sel2)
            e.tensor_tensor(selb[:, :, :], sel1, sel2, ALU.add).then_inc(S["m"], 1)
            yield
            w(e, "cw", g)
            e.tensor_tensor(exw[:, :, 0:E], Lg[:, :, :], wide(m1), ALU.subtract)
            yield
            e.tensor_tensor(exw[:, :, E], m2, m1, ALU.subtract).then_inc(S["e1"], 1)

        def sigm(g):
            @step("act")
            def _(e):
                w(e, "e1", g + 1)
                w(e, "cw", g)
                e.activation(sgw[:, :, :], exw[:, :, :], ACT.Sigmoid).then_inc(S["e2"], 1)

        def cweights(e, g):
            hm = h2all[:, 4 * g:4 * g + 4, :]
            w(e, "e2", g + 1)
            yield from lk(e, e.tensor_scalar(exw[:, :, :], sgw[:, :, :], -1.0, 1.0, ALU.mult, ALU.add), "ch3")
            yield from lk(e, e.reciprocal(exw[:, :, :], exw[:, :, :]), "ch3")
            yield from lk(e, e.tensor_tensor(exw[:, :, :], sgw[:, :, :], exw[:, :, :], ALU.mult), "ch3")
            yield from lk(e, e.tensor_reduce(wsum[:, 0, :], exw[:, :, 0:E], AX, ALU.add), "ch3")
            yield from lk(e, e.scalar_tensor_tensor(wsum[:, 1, :], wsum[:, 0, :], 1e-8, exw[:, :, E],
                                                    ALU.mult, ALU.add), "ch3")
            yield from lk(e, e.tensor_scalar(wsum[:, 1, :], wsum[:, 1, :], 1.0, None, ALU.add), "ch3")
            yield from lk(e, e.reciprocal(hm[:, :, D], wsum[:, 1, :]), "ch3")
            e.tensor_tensor(hm[:, :, D + 1], exw[:, :, E], hm[:, :, D], ALU.mult).then_inc(S["cw"], 1)

        def rank(g):
            @step("pe")
            def _(e):
                w(e, "m", g + 1)
                w(e, "cs", g)
                w(e, "cst", 7)
                flat = selb[:, :, :].rearrange("p j e -> p (j e)")
                if g >= NG - 2:
                    w(e, "so", 4 * NG)
                    w(e, "rr", g)
                o = at_places(g)
                e.matmul(o, upper[:, :], flat, start=True, stop=False, skip_group_check=True)
                for q in range(1, 4):
                    e.matmul(o[:, E * q:4 * E], ones[:, :], flat[:, 0:E * (4 - q)], start=False, stop=False,
                             skip_group_check=True)
                e.matmul(o, ones[:, :], bc(csum[:, :], 4), start=False, stop=True,
                         skip_group_check=True).then_inc(S["rk"], 1)

        def place(e, g):
            w(e, "rk", g + 1)
            sel1, sel2 = (sel[:, q, :, :] for q in range(2))
            e.tensor_tensor(rt[:, 2, :, :], at_places(g).rearrange("p (j e) -> p j e", j=4), ebase, ALU.add)\
                .then_inc(S["rr"], 1)
            yield
            w(e, "rr", g + 1)
            if g == NG - 2:
                e.tensor_scalar(lateint[0:1, 0:1], rt[0:1, 2, 0, 0:1], float(TE), None, ALU.is_lt)\
                    .then_inc(S["late"], 1)
                yield
            yield from lk(e, e.tensor_tensor(rt[:, 3, :, :], rt[:, 2, :, :], sel1, ALU.mult), "ch2")
            hm = h2all[:, 4 * g:4 * g + 4, :]
            w(e, "met", 7)
            yield from lk(e, e.tensor_reduce(hm[:, :, D + 2], rt[:, 3, :, :], AX, ALU.add), "ch2")
            yield from lk(e, e.tensor_tensor(rt[:, 3, :, :], rt[:, 2, :, :], sel2, ALU.mult), "ch2")
            yield from lk(e, e.tensor_reduce(hm[:, :, D + 3], rt[:, 3, :, :], AX, ALU.add), "ch2")
            e.tensor_copy(pos[:, :, 4 * g:4 * g + 4], hm[:, :, D + 2:D + 4].rearrange("p j q -> p q j"))\
                .then_inc(S["pos"], 1)
            w(e, "cs", g)
            yield from lk(e, e.tensor_reduce(kf[:, :], selb[:, :, :].rearrange("p j e -> p e j"), AX, ALU.add), "ch2")
            e.tensor_tensor(csum[:, :], csum[:, :], kf[:, :], ALU.add).then_inc(S["cs"], 1)

        def empties_go(e, n0, n1):
            t, x, v = (prex[:, q, :, n0:n1] for q in range(1, 4))
            dmp = dump[:, :, n0:n1]
            link(e, e.tensor_tensor(t, x, dmp, ALU.subtract))
            link(e, e.tensor_tensor(t, t, v, ALU.mult))
            link(e, e.tensor_tensor(t, t, dmp, ALU.add))
            e.tensor_scalar(prei[:, :, n0:n1], t, float(DW // MW), float(D // MW), ALU.mult, ALU.add)\
                .then_inc(S["prei"], 1)

        def empties():
            @step("dve")
            def _(e):
                def wide(v):
                    return v.unsqueeze(2).to_broadcast([128, 2, E])

                x, v = prex[:, 2, :, :], prex[:, 3, :, :]
                link(e, e.tensor_tensor(x, rt[:, 2, 0:2, :], wide(tq), ALU.subtract))
                link(e, e.tensor_tensor(v, x, ebase[:, 0:2, :], ALU.is_ge))
                link(e, e.scalar_tensor_tensor(v, selb[:, 0:2, :], 0.5, v, ALU.is_lt, ALU.mult))
                empties_go(e, 0, 1)

            @step("pool")
            def _(e):
                w(e, "prei", 1)
                w(e, "zf", 16 * E)
                empties_put(e, 0)

        def empties_where(e):
            a, x, v = (prex[:, q, :, :] for q in (0, 2, 3))
            link(e, e.tensor_tensor(a, ebase[:, 0:2, :], bc(nf[:, 0, :], 2), ALU.add))
            link(e, e.tensor_tensor(a, x, a, ALU.is_ge))
            link(e, e.tensor_tensor(v, v, a, ALU.mult))
            empties_go(e, 1, E)

        def empties_put(e, n):
            for j in range(2):
                e.indirect_dma_start(out=Xm, out_offset=bass.IndirectOffsetOnAxis(ap=prei[:, j, n:n + 1], axis=0),
                                     in_=prem[:, j, :], in_offset=None).then_inc(S["pre1" if n else "pre0"], 16)

        def scat_of(g):
            return "scat0" if g < 4 else "scat1" if g < NG - 2 else "scat2"

        def scatter(g, half):
            @step("pool")
            def _(e):
                w(e, "pos", g + 1)
                w(e, "cw", g + 1)
                w(e, "pre0", 32)
                w(e, "zf", 16 * E)
                for j in range(4 * g + 2 * half, 4 * g + 2 * half + 2):
                    for p in (pos[:, 0, :], pos[:, 1, :]):
                        e.indirect_dma_start(out=Xd, out_offset=bass.IndirectOffsetOnAxis(ap=p[:, j:j + 1], axis=0),
                                             in_=h2all[:, j, :], in_offset=None).then_inc(S[scat_of(g)], 16)

        def counts():
            @step("pe")
            def _(e):
                w(e, "cs", NG)
                e.matmul(yb[1][:, 0:E], ones[:, :], csum[:, :], start=True, stop=True).then_inc(S["nc"], 1)

            @step("dve")
            def _(e):
                w(e, "nc", 1)
                link(e, e.tensor_copy(nf[:, 0, :], yb[1][:, 0:E]))
                link(e, e.tensor_scalar(nf[:, 1, :], nf[:, 0, :], -128.0, None, ALU.add))
                e.tensor_scalar(nmint[:, :], nf[:, 1, :], 0.0, None, ALU.max).then_inc(S["kr"], 1)
                link(e, e.tensor_tensor(ncmp[:, :, :, :], nf[:, :, :].unsqueeze(3).to_broadcast([128, 2, E, 14]),
                                        thr.unsqueeze(1).to_broadcast([128, 2, E, 14]), ALU.is_gt))
                link(e, e.tensor_reduce(kf2[:, :, :], ncmp[:, :, :, :], AX, ALU.add))
                link(e, e.scalar_tensor_tensor(kf2[:, 0, :], kf2[:, 0, :], 2.0, kf2[:, 1, :], ALU.add, ALU.add))
                link(e, e.tensor_tensor(kf2[:, 0, :], kf2[:, 0, :], iof[:, 196:204], ALU.mult))
                link(e, e.tensor_reduce(kf[:, 0:2], kf2[:, 0, :].rearrange("p (h i) -> p h i", h=2), AX, ALU.add))
                e.tensor_copy(kpk[:, :], kf[:, 0:2]).then_inc(S["kr"], 1)
                link(e, e.tensor_reduce(kf[:, 2:3], nf[:, 1, :], AX, ALU.min))
                e.tensor_scalar(few[:, :], kf[:, 2:3], 0.0, None, ALU.is_lt).then_inc(S["few"], 1)

        def split_hi(e, n, q):
            r = slice(q * 512, (q + 1) * 512)
            if q in (0, 4):
                w(e, f"raw{n % 2}", 32 * (n // 2 + 1))
            if q < 4 and n:
                e.tensor_copy(SH[n % 2][:, r], wraw[n % 2][:, r]).then_inc(S["sph"], 1)
            else:
                e.activation(SH[n % 2][:, r], wraw[n % 2][:, r], ACT.Copy).then_inc(S["sph" if q < 4 else "sph2"], 1)

        def split_lo(e, n, q):
            r = slice(q * 512, (q + 1) * 512)
            w(e, "sph" if q < 4 else "sph2", 4 * n + q % 4 + 1)
            e.tensor_tensor(SL[n % 2][:, r], wraw[n % 2][:, r], SH[n % 2][:, r].bitcast(F32), ALU.subtract)\
                .then_inc(S["spl" if q < 5 else "spl2"], 1)

        def split_done(e, n):
            w(e, "spl", 5 * (n + 1))
            w(e, "spl2", 3 * (n + 1))

        def counts_of(e):
            rs = [e.alloc_register(f"counts{h}") for h in range(2)]
            for h in range(2):
                e.reg_load(rs[h], kpk[0:1, h:h + 1])
            return rs

        def count_of(e, rs, n):
            k, half = (e.alloc_register(f"{name}{n}") for name in ("tiles", "half"))
            e.reg_alu(half, rs[n // (E // 2)], 5 * (n % (E // 2)), ALU.logical_shift_right)
            e.reg_alu(k, half, 1, ALU.logical_shift_right)
            e.reg_alu(k, k, 15, ALU.bitwise_and)
            e.reg_alu(half, half, 1, ALU.bitwise_and)
            return e.snap(k, min_val=1, max_val=CAP // TE - 1), half

        def more_tiles(e, rs, n, tile):
            k, half = count_of(e, rs, n)
            with e.Fori(0, k):
                tile(False, 2)
            with e.If_ne(half, 0):
                tile(False, 1)

        def tiles(e, rs, n, tile):
            tile(True, 2)
            more_tiles(e, rs, n, tile)

        def counter(e, engine, names):
            rl = {k: e.alloc_register(f"{engine}_{k}") for k in names}
            for r in rl.values():
                e.reg_mov(r, 0)

            def due(name, by):
                e.reg_add(rl[name], rl[name], by)
                e.wait_ge(S[name], rl[name])
                if engine in ("pool", "sp"):
                    e.sem_inc(S["tick_" + engine], 1)
            return rl, due

        def pe_experts(e):
            rl, due = counter(e, "pe", ("g", "hlo", "yev", "xin", "fl"))

            def turn():
                due("xin", 32)
                for k in range(2):
                    for j in range(2):
                        i = e.transpose(tp[k][:, j * 128:(j + 1) * 128], xin[:, j, k * 128:(k + 1) * 128],
                                        ident[:, :])
                    i.then_inc(S["tp2"], 1)

            e.reg_mov(rl["hlo"], 2)
            e.sem_inc(S["l2"], NF)
            turn()
            ks = []
            for n in range(E):
                s = n % 2
                w1h, w1l = (t[s][:, 0:2048].rearrange("p (c n) -> p c n", c=2) for t in (SH, SL))
                w2h, w2l = (t[s][:, 2048:4096].rearrange("p (c n) -> p c n", c=NF) for t in (SH, SL))
                split_done(e, n)

                def layer1(f, parts):
                    due("g", 1)
                    for k in range(2):
                        for t, (a, b) in enumerate(((w1h, fh), (w1h, fl), (w1l, fh))):
                            i = e.matmul(mm[f % 4][:, 0:TE], a[:, k, f * 128:(f + 1) * 128], b[:, k, :],
                                         start=(k == 0 and t == 0), stop=(k == 1 and t == 2))
                    i.then_inc(S["l1"], 1)

                def layer2(f, parts):
                    if f == 0:
                        due("yev", 1)
                    due("hlo", 1)
                    for j in range(parts):
                        for t, (a, b) in enumerate(((hh, w2h), (hh, w2l), (hl, w2h))):
                            i = e.matmul(yb[0][:, j * D:(j + 1) * D], a[:, f, j * 128:(j + 1) * 128], b[:, f, :],
                                         start=(f == 0 and j == 0 and t == 0), stop=(f == NF - 1 and t == 2),
                                         skip_group_check=True)
                    i.then_inc(S["l2"], 1)

                def tile(first, parts):
                    due("fl", 2)
                    for f in range(NF):
                        layer1(f, parts)
                        if f >= 4:
                            layer2(f - 4, parts)
                    layer2(NF - 4, parts)
                    if first and n == 0:
                        w(e, "kr", 2)
                        ks.extend(counts_of(e))
                    turn()
                    for f in range(NF - 3, NF):
                        layer2(f, parts)

                tiles(e, ks, n, tile)

        def act_experts(e):
            rl, due = counter(e, "act", ("l1", "hlo", "l2", "tp2"))

            def part():
                for k in range(2):
                    due("tp2", 1)
                    e.activation(fh[:, k, :], tp[k][:, 0:TE], ACT.Copy).then_inc(S["fh"], 1)

            e.reg_mov(rl["tp2"], 2)
            e.sem_inc(S["g"], 4)
            part()
            w(e, "kr", 2)
            e.activation(b1T[:, :], vT[:, 0:64], ACT.Copy).then_inc(S["b1T"], 1)
            ks = counts_of(e)
            w(e, "b1T", 1)
            for n in range(E):
                def tile(first, parts):
                    c_ = slice(0, 128 * parts)
                    for f in range(NF):
                        due("l1", 1)
                        due("hlo", 1)
                        due("l2", 1)
                        bias = b1T[:, n * NF + f:n * NF + f + 1]
                        e.activation(h32[:, f % 2, c_], mm[f % 4][:, c_], ACT.Gelu_apprx_tanh, bias=bias)
                        e.activation(hh[:, f, c_], mm[f % 4][:, c_], ACT.Gelu_apprx_tanh, bias=bias)\
                            .then_inc(S["g"], 1)
                        if first and n + 1 < E and f >= 4:
                            split_hi(e, n + 1, f)
                    part()

                tiles(e, ks, n, tile)

        def dve_experts(e):
            rl, due = counter(e, "dve", ("g", "fh", "l2", "yf", "xin", "gg", "ch3"))
            e.reg_mov(rl["g"], 4)
            e.reg_mov(rl["l2"], NF)
            e.reg_mov(rl["ch3"], count["ch3"])

            def own(ins):
                ins.then_inc(S["ch3"], 1)

            def part():
                for k in range(2):
                    due("fh", 1)
                    e.tensor_tensor(fl[:, k, :], tp[k][:, 0:TE], fh[:, k, :].bitcast(F32), ALU.subtract)\
                        .then_inc(S["fl"], 1)

            def columns():
                due("xin", 32)
                e.tensor_copy(xm[:, :, :], xin[:, :, D:DW]).then_inc(S["ma"], 1)

            e.sem_inc(S["hlo"], 2)
            e.sem_inc(S["yev"], 1)
            ks = []
            part()
            columns()
            empties_where(e)
            for n in range(E):
                if n == 0:
                    w(e, "b2", 16)

                def high(f, c_):
                    due("g", 1)
                    e.tensor_tensor(hl[:, f, c_], h32[:, f % 2, c_], hh[:, f, c_].bitcast(F32), ALU.subtract)\
                        .then_inc(S["hlo"], 1)

                def tile(first, parts):
                    a, b, c_ = (wsl[:, q, :, :] for q in range(3))
                    place = xm[:, :, 2:4]
                    small = {
                        1: lambda: e.tensor_tensor(a, place, nom[:, :].unsqueeze(2).to_broadcast([128, 2, 2]),
                                                   ALU.is_ge),
                        2: lambda: e.scalar_tensor_tensor(b, place, float((n + 1) * CAP), a, ALU.is_lt, ALU.mult),
                        3: lambda: e.tensor_tensor(c_, b, xm[:, :, 0:2], ALU.mult),
                        4: lambda: e.tensor_reduce(wB[:, :], c_, AX, ALU.add),
                        5: lambda: e.tensor_scalar(nom[:, :], nom[:, :], float(TE), None, ALU.add),
                    }
                    if first:
                        own(e.tensor_scalar(nom[:, :], nom0, float(n * CAP), None, ALU.add))
                        due("ch3", 1)
                    for f in range(NF):
                        high(f, slice(0, 128 * parts))
                        if f in small:
                            if f > 1:
                                due("ch3", 1)
                            own(small[f]())
                        if first and n == 0 and f == 4:
                            ks.extend(counts_of(e))
                        if first and n + 1 < E:
                            if f < 4:
                                split_hi(e, n + 1, f)
                            if f in (2, 3, 5, 6):
                                split_lo(e, n + 1, (2, 3, 5, 6).index(f))
                    if first and n + 1 < E:
                        split_lo(e, n + 1, 4)
                    due("ch3", 1)
                    part()
                    due("yf", 1)
                    own(e.tensor_copy(tokb[:, :], xm[:, :, 4].bitcast(I32)))
                    due("ch3", 1)
                    due("gg", 32)
                    columns()
                    due("l2", NF)
                    own(e.tensor_tensor(ysb[:, 0:parts, :],
                                        yb[0][:, 0:parts * D].rearrange("p (j d) -> p j d", j=parts),
                                        bc(b2b[:, n, :], parts), ALU.add))
                    due("ch3", 1)
                    for j in range(parts):
                        i = e.scalar_tensor_tensor(ysb[:, j, :], ysb[:, j, :], wB[:, j:j + 1], gbr[:, j, :],
                                                   ALU.mult, ALU.mult)
                    i.then_inc(S["yev"], 1)

                tile(True, 2)
                more_tiles(e, ks, n, tile)

        def sp_experts(e):
            r_pos, r_at, r_last = (e.alloc_register("sp_" + k) for k in ("pos", "at", "last"))
            rl, due = counter(e, "sp", ("tp2", "ma"))

            def load(rows_of):
                due("tp2", 2)
                due("ma", 1)
                for j in range(2):
                    e.dma_start(xin[:, j, :], rows_of(j)).then_inc(S["xin"], 16)

            r_late = e.alloc_register("sp_late")
            w(e, "late", 1)
            e.reg_load(r_late, lateint[0:1, 0:1])
            e.reg_mov(r_last, CAP - 128)
            w(e, "scat0", 16 * 8 * 4)
            w(e, "scat1", 16 * 8 * 2)
            w(e, "pre0", 32)
            with e.If_ne(r_late, 0):
                w(e, "scat2", 16 * 8 * 2)
                w(e, "kr", 1)
                e.reg_load(r_last, nmint[0:1, 0:1])
            e.sem_inc(S["tp2"], 2)
            e.sem_inc(S["ma"], 1)
            for n in range(E):
                if n == 1:
                    w(e, "filled", 1)
                if n:
                    e.reg_load(r_last, nmint[0:1, n:n + 1])
                e.reg_mov(r_pos, 0)

                def rows_of(j):
                    e.reg_alu(r_at, r_pos, r_last, ALU.min)
                    e.reg_add(r_at, r_at, n * CAP)
                    e.reg_add(r_pos, r_pos, 128)
                    return Xd[bass.ds(e.snap(r_at, min_val=0, max_val=E * CAP - 128), 128), :]

                def tile(first, parts):
                    load(rows_of)
                    if first and n == 0:
                        w(e, "kr", 2)
                        e.reg_load(r_last, nmint[0:1, n:n + 1])
                    if first and n + 2 < E:
                        split_done(e, n)
                        load_w1(e, n + 2)

                if n == 0:
                    tile(True, 2)
                    ks = counts_of(e)
                    w(e, "scat2", 16 * 8 * 2)
                    more_tiles(e, ks, n, tile)
                else:
                    tiles(e, ks, n, tile)
                if n + 2 < E:
                    load_w2(e, n + 2)
            load(lambda j: Xd[0:128, :])

        def pool_experts(e):
            rl, due = counter(e, "pool", ("yev", "ma", "yst", "gg"))
            w(e, "kr", 2)
            ks = counts_of(e)

            def gather():
                due("ma", 1)
                for j in range(2):
                    e.indirect_dma_start(out=gbr[:, j, :], out_offset=None, in_=modd.rearrange("b (n d) -> (b n) d", d=D),
                                         in_offset=bass.IndirectOffsetOnAxis(ap=xm[:, j, 5:6].bitcast(I32), axis=0))\
                        .then_inc(S["gg"], 16)

            def add(j):
                e.indirect_dma_start(out=out_rows, out_offset=bass.IndirectOffsetOnAxis(ap=tokb[:, j:j + 1], axis=0),
                                     in_=ysb[:, j, :], in_offset=None, compute_op=ALU.add).then_inc(S["yst"], 16)

            e.sem_inc(S["yf"], 1)
            e.reg_mov(rl["yev"], 1)
            w(e, "x2w0", 16 * (NG // 2))
            w(e, "x2w1", 16 * (NG // 2))
            e.reg_mov(rl["ma"], 1)
            gather()
            w(e, "prei", 2)
            w(e, "few", 1)
            r_few = e.alloc_register("pool_few")
            e.reg_load(r_few, few[0:1, 0:1])
            with e.If_ne(r_few, 0):
                for n in range(1, E):
                    empties_put(e, n)
                w(e, "pre1", 32 * (E - 1))
            e.sem_inc(S["filled"], 1)
            for n in range(E):
                def tile(first, parts):
                    if first and n + 1 < E:
                        for q in range(5, 8):
                            split_lo(e, n + 1, q)
                    due("yev", 1)
                    add(0)
                    gather()
                    due("yst", 16)
                    if parts == 2:
                        add(1)
                        due("yst", 16)
                    e.sem_inc(S["yf"], 1)

                tiles(e, ks, n, tile)
            due("gg", 32)

        def split_first():
            @step("act")
            def _(e):
                w(e, "mm", 16 * NG)
                for q in range(8):
                    split_hi(e, 0, q)

            @step("pool")
            def _(e):
                for q in range(5, 8):
                    split_lo(e, 0, q)

        def split_rest(q0, q1):
            @step("dve")
            def _(e):
                for q in range(q0, q1):
                    split_lo(e, 0, q)

        def second_expert():
            @step("sp")
            def _(e):
                w(e, "scat0", 16 * 8 * 4)
                load_expert(e, 1)
                w(e, "z2", NG - 1)
                w(e, "z2_", 1)
                w(e, "x2w0", 16 * (NG // 2))
                w(e, "x2w1", 16 * (NG // 2))
                e.dma_start(b2b[:, :, :].rearrange("p e d -> p (e d)"),
                            b2.rearrange("e d -> (e d)").partition_broadcast(128)).then_inc(S["b2"], 16)

        def do(g, *parts):
            for fn, *args in parts:
                if 0 <= g < NG:
                    fn(g, *args)

        def dve(*chains):
            chains = [(fn, g) for g, fn in chains if 0 <= g < NG]

            @step("dve")
            def _(e):
                weave(*(fn(e, g) for fn, g in chains))

        setup()
        dve((0, ln1_stats))
        mod_first()
        ln1_h(0)
        for k in range(2):
            weights_hi(0, k)
        mod_rows(0)
        for k in range(2):
            weights_lo(0, k)
        ln1_sq(0)
        for k in range(2):
            weights_hi(1, k)
        dve((0, ln1_norm))
        ln1_xn(0)
        mod_rows(1)
        mod_rows(2)
        for k in range(2):
            weights_lo(1, k)
        xt(0)
        for g in range(NG):
            last = g == NG - 1
            if g == 2:
                token_columns()
            do(g - 3, (turn_h,))
            dve((g + 1, ln1_stats))
            if last:
                dve((g - 2, ln2_stats))
            do(g - 4, (scatter, 1))
            do(g, (main, 0))
            if g == 0:
                weights_out()
                mod_guards()
            do(g - 1, (split_o, 3), (project, 2))
            do(g - 3, (logits,))
            do(g + 1, (ln1_h,))
            if last:
                ln2_h(g - 2)
                dve((g - 3, top2))
            else:
                dve((g - 2, ln2_stats), (g - 3, top2))
            do(g, (main, 1), (split_o, 0))
            do(g - 1, (project, 3))
            do(g - 3, (rank,))
            do(g + 1, (ln1_sq,))
            do(g - 3, (sigm,))
            if not last:
                do(g - 2, (ln2_h,))
            dve((g + 1, ln1_norm), (g - 3, place), (g - 3, cweights))
            if g == 3:
                empties()
            do(g - 1, (post,))
            if last:
                turn_h(g - 2)
            do(g, (main, 2), (split_o, 1), (project, 0))
            do(g + 1, (ln1_xn,))
            do(g - 3, (scatter, 0))
            do(g - 1, (add_x,))
            if last:
                logits(g - 2)
                dve((g - 1, ln2_stats), (g - 2, top2))
                sigm(g - 2)
            do(g, (main, 3, lambda: do(g + 1, (xt,))), (split_o, 2), (project, 1))

        g = NG - 1
        split_o(g, 3)
        scatter(g - 3, 1)
        ln2_h(g - 1)
        rank(g - 2)
        project(g, 2)
        project(g, 3)
        dve((g - 2, place), (g - 2, cweights))
        post(g)
        add_x(g)
        second_expert()
        scatter(g - 2, 0)
        scatter(g - 2, 1)
        split_first()
        turn_h(g - 1)
        logits(g - 1)
        dve((g, ln2_stats))
        ln2_h(g)
        turn_h(g)
        dve((g - 1, top2))
        rank(g - 1)
        sigm(g - 1)
        logits(g)
        dve((g - 1, place), (g - 1, cweights))
        split_rest(0, 2)
        scatter(g - 1, 0)
        scatter(g - 1, 1)
        dve((g, top2))
        rank(g)
        sigm(g)
        dve((g, place), (g, cweights))
        scatter(g, 0)
        scatter(g, 1)
        split_rest(2, 5)
        counts()

        @step("act")
        def _(e):
            e.activation(gl[:, :], zcol[:, :], ACT.Gelu_apprx_tanh)

        for name, fn in (("sp", sp_experts), ("pool", pool_experts), ("act", act_experts), ("pe", pe_experts),
                         ("dve", dve_experts)):
            steps.append((name, fn))
        def emit(name, e):
            for engine, fn in steps:
                if engine == name:
                    fn(e)

        block = ctx.enter_context(nc.Block())

        @block.sync
        def _(e):
            emit("sp", e)

        @block.gpsimd
        def _(e):
            emit("pool", e)

        @block.scalar
        def _(e):
            emit("act", e)

        @block.tensor
        def _(e):
            emit("pe", e)

        @block.vector
        def _(e):
            emit("dve", e)


INPUTS = ("L0_attn_x", "L0_attn_rms_scale", "L0_attn_split_scale", "L0_attn_W_K", "L0_attn_W_ugg", "L0_attn_W_out",
          "L0_ffn_Wg", "L0_ffn_bg", "L0_ffn_W1", "L0_ffn_b1", "L0_ffn_W2", "L0_ffn_b2", "L0_c", "L0_wmod")


def kernel(**inputs):
    import numpy as np
    import concourse.bacc as bacc
    from concourse.bass_utils import run_bass_kernel_spmd as run

    nc = bacc.Bacc("TRN2", target_bir_lowering=False, num_devices=1)
    arrays, args = {}, []
    for name in INPUTS:
        a = np.ascontiguousarray(inputs[name])
        arrays["in_" + name] = a
        args.append(nc.dram_tensor("in_" + name, a.shape, mybir.dt.from_np(a.dtype), kind="ExternalInput").ap())
    out = nc.dram_tensor("out_x", (NB, TOK // NB, D), F32, kind="ExternalOutput").ap()
    build(nc, *args, out)
    r = run(nc, [arrays], core_ids=[0])
    return r.results[0]["out_x"]
```
